# Optimizing a Trainium2 kernel written in Bass

```python
import numpy as np
import jax
import jax.numpy as jnp

def _softmax(x, axis=-1):
    return jax.nn.softmax(x, axis=axis)

def _gelu(x):
    return jax.nn.gelu(x, approximate=True)

def _silu(x):
    return jax.nn.silu(x)

def _sigmoid(x):
    return jax.nn.sigmoid(x)

def _layernorm(x, axis=-1, eps=1e-05):
    m = jnp.mean(x, axis=axis, keepdims=True)
    v = jnp.var(x, axis=axis, keepdims=True)
    return (x - m) / jnp.sqrt(v + eps)

def _scatter_add(tgt, idx, src, axis=0):
    return tgt.at[idx].add(src)

def _segment_sum(src, seg, n):
    return jax.ops.segment_sum(src, seg, n)
kernel_name = 'mk_vit_tower_cls_d1_tok_img768_r4_fd944c'

def setup_inputs(seed: int=0):
    np.random.seed(seed)
    _w = jnp.asarray

    def _rec_inputs():
        import jax
        import jax.numpy as jnp
        _rk = jax.random.key(seed)
        x = -0.000356955 + 1 * jax.random.normal(jax.random.fold_in(_rk, 1), (16, 3, 96, 96), jnp.float32)
        cls_tok = 0.02 * jax.random.normal(jax.random.fold_in(_rk, 5), (1, 1, 192), jnp.float32)
        return (x, cls_tok)
    x, cls_tok = _rec_inputs()

    def _L0_tok_setup():
        import jax, jax.numpy as jnp
        import numpy as np
        PATCH = 16
        key = jax.random.key(seed)
        k1, k2, k3 = jax.random.split(key, 3)
        x = jax.random.normal(k1, (128, 3, 224, 224), dtype=jnp.float32)
        W = jax.random.normal(k2, (192, 3, PATCH, PATCH), dtype=jnp.float32) * 0.02
        b = jax.random.normal(k3, (192,), dtype=jnp.float32) * 0.02
        return {'x': x, 'W': W, 'b': b}
    _L0_tok_all = _L0_tok_setup()
    _L0_tok_in = {k: v for k, v in _L0_tok_all.items() if k in ('W', 'b')}
    del _L0_tok_all

    def _L0_attn_setup():
        import jax, jax.numpy as jnp
        import numpy as np
        MODEL_DIM = 192
        HEADS = 12
        HEAD_DIM = MODEL_DIM // HEADS
        SEQ = 512

        def _rope_tables(seq_len, d):
            i = np.arange(d // 2, dtype=np.float64)
            theta = 10000.0 ** (-2.0 * i / d)
            m = np.arange(1, seq_len + 1, dtype=np.float64)[:, None]
            m_theta = np.repeat(m * theta[None, :], 2, axis=-1)
            return (jnp.asarray(np.cos(m_theta), jnp.float32), jnp.asarray(np.sin(m_theta), jnp.float32))

        def _shuffle(x):
            b, t, d = x.shape
            xp = x.reshape(b, t, d // 2, 2)
            xp = jnp.stack([-xp[..., 1], xp[..., 0]], axis=-1)
            return xp.reshape(b, t, d)

        def _rope(x, cos, sin):
            t = x.shape[-2]
            return x * cos[:t][None] + _shuffle(x) * sin[:t][None]
        key = jax.random.key(seed)
        kx, kq, kk, kv, ko = jax.random.split(key, 5)
        x = jax.random.normal(kx, (4, SEQ, MODEL_DIM), jnp.float32)
        std = 0.02
        W_q = jax.random.normal(kq, (MODEL_DIM, MODEL_DIM), jnp.float32) * std
        W_k = jax.random.normal(kk, (MODEL_DIM, MODEL_DIM), jnp.float32) * std
        W_v = jax.random.normal(kv, (MODEL_DIM, MODEL_DIM), jnp.float32) * std
        W_o = jax.random.normal(ko, (MODEL_DIM, MODEL_DIM), jnp.float32) * std
        return {'x': x, 'W_q': W_q, 'W_k': W_k, 'W_v': W_v, 'W_o': W_o}
    _L0_attn_all = _L0_attn_setup()
    _L0_attn_in = {k: v for k, v in _L0_attn_all.items() if k in ('W_q', 'W_k', 'W_v', 'W_o')}
    del _L0_attn_all

    def _L0_ffn_setup():
        import jax, jax.numpy as jnp
        import numpy as np
        B, T, D = (4, 512, 192)
        E, F, K = (8, 4 * 192, 2)
        key = jax.random.key(seed)
        ks = jax.random.split(key, 5)
        s = 0.02
        return {'x': jax.random.normal(ks[0], (B, T, D), dtype=jnp.float32), 'Wg': jax.random.normal(ks[1], (D, E), dtype=jnp.float32) * s, 'bg': jnp.zeros((E,), dtype=jnp.float32), 'W1': jax.random.normal(ks[2], (E, D, F), dtype=jnp.float32) * s, 'b1': jnp.zeros((E, F), dtype=jnp.float32), 'W2': jax.random.normal(ks[3], (E, F, D), dtype=jnp.float32) * s, 'b2': jnp.zeros((E, D), dtype=jnp.float32)}
    _L0_ffn_all = _L0_ffn_setup()
    _L0_ffn_in = {k: v for k, v in _L0_ffn_all.items() if k in ('Wg', 'bg', 'W1', 'b1', 'W2', 'b2')}
    del _L0_ffn_all
    return {'x': x, 'cls_tok': cls_tok, 'L0_tok_W': _L0_tok_in['W'], 'L0_tok_b': _L0_tok_in['b'], 'L0_attn_W_q': _L0_attn_in['W_q'], 'L0_attn_W_k': _L0_attn_in['W_k'], 'L0_attn_W_v': _L0_attn_in['W_v'], 'L0_attn_W_o': _L0_attn_in['W_o'], 'L0_ffn_Wg': _L0_ffn_in['Wg'], 'L0_ffn_bg': _L0_ffn_in['bg'], 'L0_ffn_W1': _L0_ffn_in['W1'], 'L0_ffn_b1': _L0_ffn_in['b1'], 'L0_ffn_W2': _L0_ffn_in['W2'], 'L0_ffn_b2': _L0_ffn_in['b2']}

def reference(x, cls_tok, L0_tok_W, L0_tok_b, L0_attn_W_q, L0_attn_W_k, L0_attn_W_v, L0_attn_W_o, L0_ffn_Wg, L0_ffn_bg, L0_ffn_W1, L0_ffn_b1, L0_ffn_W2, L0_ffn_b2):
    import jax
    import jax.numpy as jnp

    def _L0_tok_ref(x, W, b):
        import jax, jax.numpy as jnp
        import numpy as np
        PATCH = 16
        B, C, H, Wd = x.shape
        E = W.shape[0]
        p = PATCH
        xp = x.reshape(B, C, H // p, p, Wd // p, p)
        out = jnp.einsum('bchpwq,ecpq->bhwe', xp, W) + b
        return out.reshape(B, H // p * (Wd // p), E)

    def _L0_attn_ref(x, W_q, W_k, W_v, W_o):
        import jax, jax.numpy as jnp
        import numpy as np
        MODEL_DIM = 192
        HEADS = 12
        HEAD_DIM = MODEL_DIM // HEADS
        SEQ = 512

        def _rope_tables(seq_len, d):
            i = np.arange(d // 2, dtype=np.float64)
            theta = 10000.0 ** (-2.0 * i / d)
            m = np.arange(1, seq_len + 1, dtype=np.float64)[:, None]
            m_theta = np.repeat(m * theta[None, :], 2, axis=-1)
            return (jnp.asarray(np.cos(m_theta), jnp.float32), jnp.asarray(np.sin(m_theta), jnp.float32))

        def _shuffle(x):
            b, t, d = x.shape
            xp = x.reshape(b, t, d // 2, 2)
            xp = jnp.stack([-xp[..., 1], xp[..., 0]], axis=-1)
            return xp.reshape(b, t, d)

        def _rope(x, cos, sin):
            t = x.shape[-2]
            return x * cos[:t][None] + _shuffle(x) * sin[:t][None]
        b, t, d = x.shape
        cos, sin = _rope_tables(t, d)
        Q = _rope(x @ W_q.T, cos, sin)
        K = _rope(x @ W_k.T, cos, sin)
        V = x @ W_v.T
        Qh = Q.reshape(b, t, HEADS, HEAD_DIM)
        Kh = K.reshape(b, t, HEADS, HEAD_DIM)
        Vh = V.reshape(b, t, HEADS, HEAD_DIM)
        scores = jnp.einsum('bthd,bshd->bhts', Qh, Kh) / jnp.sqrt(jnp.float32(HEAD_DIM))
        mask = jnp.triu(jnp.ones((t, t), bool), k=1)
        scores = jnp.where(mask[None, None], -jnp.inf, scores)
        attn = jax.nn.softmax(scores, axis=-1)
        out = jnp.einsum('bhts,bshd->bthd', attn, Vh).reshape(b, t, d)
        return out @ W_o.T

    def _L0_ffn_ref(x, Wg, bg, W1, b1, W2, b2):
        import jax, jax.numpy as jnp
        import numpy as np
        B, T, D = (4, 512, 192)
        E, F, K = (8, 4 * 192, 2)
        b, t, d = x.shape
        x_flat = x.reshape(-1, d)
        n = x_flat.shape[0]
        gates = jax.nn.softmax(x_flat @ Wg + bg, axis=-1)
        topk_g, topk_i = jax.lax.top_k(gates, K)
        combine = jnp.zeros((n, W1.shape[0]), dtype=gates.dtype)
        combine = combine.at[jnp.arange(n)[:, None], topk_i].add(topk_g)
        h = jnp.einsum('nd,edf->enf', x_flat, W1) + b1[:, None, :]
        h = jax.nn.gelu(h, approximate=False)
        y = jnp.einsum('enf,efd->end', h, W2) + b2[:, None, :]
        out = jnp.einsum('ne,end->nd', combine, y)
        return out.reshape(b, t, d)
    h = _L0_tok_ref(x, L0_tok_W, L0_tok_b)
    h = jnp.concatenate([jnp.broadcast_to(cls_tok, (h.shape[0], 1, h.shape[2])), h], axis=1)
    h = h + _L0_attn_ref(_layernorm(h, axis=-1), L0_attn_W_q, L0_attn_W_k, L0_attn_W_v, L0_attn_W_o)
    h = h + _L0_ffn_ref(_layernorm(h, axis=-1), L0_ffn_Wg, L0_ffn_bg, L0_ffn_W1, L0_ffn_b1, L0_ffn_W2, L0_ffn_b2)
    return h

_drawn_inputs = setup_inputs


def setup_inputs(seed=0):
    import zlib

    import numpy as np

    out = dict(_drawn_inputs(seed))
    spreads = {'L0_ffn_bg': (0.0, 0.292), 'L0_ffn_b1': (0.0, 0.584), 'L0_ffn_b2': (0.0, 0.1)}
    factors = {'L0_attn_W_q': 8.0, 'L0_attn_W_k': 8.0}
    for name, (base, spread) in spreads.items():
        noise = np.random.default_rng([zlib.crc32(name.encode()), seed]).standard_normal(out[name].shape)
        drawn = base * np.exp(spread * noise) if base else spread * noise
        out[name] = jnp.asarray(drawn.astype(out[name].dtype))
    for name, factor in factors.items():
        out[name] = (out[name] * factor).astype(out[name].dtype)
    return out
```

```python
import concourse.bass as bass
from concourse import mybir
from contextlib import ExitStack

F32 = mybir.dt.float32
BF16 = mybir.dt.bfloat16
FP16 = mybir.dt.float16
U32 = mybir.dt.uint32
ALU = mybir.AluOpType
ACT = mybir.ActivationFunctionType
AX = mybir.AxisListType

IMAGES = 16
SEQ = 37
GROUP = 3
TOK = GROUP * SEQ
N = IMAGES * SEQ
TILES = -(-N // TOK)
ROWS = [min(TOK, N - t * TOK) for t in range(TILES)]
D = 192
DA, DB = 128, D - 128
HEADS, HD = 12, 16
HG = 4
GROUPS = HEADS // HG
KC = 6
E = 8
F = 768
FC = F // 128
HALF = N // 2
EPS = 1e-5


def vit_block(nc, patches, w_tok, tok_rows, tok_sel, w_qkv_a, w_qkv_b, rope_cos, rope_sin, mask,
              ident, ident_half, head_mask, w_o_a, w_o_b, w_g_a, w_g_b, iota8, w1_a, w1_b, b1, w2, b2, out):
    ctx = ExitStack()
    with ctx:
        def sb(name, shape, dt=F32):
            return ctx.enter_context(nc.sbuf_tensor(name, shape, dt))

        def sem(name):
            return ctx.enter_context(nc.semaphore(name))

        bank = [ctx.enter_context(nc.psum_tensor(f"bank{i}", [128, 512], F32)) for i in range(8)]

        wtok_sb = sb("wtok_sb", [128, KC, D])
        tokrows_sb = sb("tokrows_sb", [2, D])
        toksel_sb = sb("toksel_sb", [2, N])
        wqkva_sb = sb("wqkva_sb", [DA, 3 * D])
        wqkvb_sb = sb("wqkvb_sb", [DB, 3 * D])
        cos_sb = sb("cos_sb", [TOK, D])
        sin_sb = sb("sin_sb", [TOK, D])
        mask_sb = sb("mask_sb", [TOK, TOK], BF16)
        ident_sb = sb("ident_sb", [128, 128])
        identh_sb = sb("identh_sb", [128, 128], BF16)
        headmask_sb = sb("headmask_sb", [128, 8])
        woa_sb = sb("woa_sb", [DA, D])
        wob_sb = sb("wob_sb", [DB, D])
        wga_sb = sb("wga_sb", [DA, E])
        wgb_sb = sb("wgb_sb", [DB + 1, E])
        iota_sb = sb("iota_sb", [128, E])
        w1a_sb = sb("w1a_sb", [DA, E, F])
        w1b_sb = sb("w1b_sb", [DB, E, F])
        b1_sb = sb("b1_sb", [128, E * FC])
        w2_sb = sb("w2_sb", [128, E, FC, D])
        b2_sb = sb("b2_sb", [E, D])

        h = sb("h", [TOK, TILES, D])
        stats = sb("stats", [TOK, TILES, 6])
        mv = sb("mv", [TOK, TILES, 2])
        veps = sb("veps", [TOK, TILES])
        lnv = sb("lnv", [TOK, TILES])
        r0 = sb("r0", [TOK, TILES])
        r1 = sb("r1", [TOK, TILES])
        r2 = sb("r2", [TOK, TILES])
        rstd = sb("rstd", [TOK, TILES])
        hn = sb("hn", [TOK, TILES, D])
        hnta = sb("hnta", [DA, 2, TOK])
        hntb = sb("hntb", [DB, 2, TOK])
        ropec = sb("ropec", [TOK, 2, 2 * D])
        ropes = sb("ropes", [TOK, 2, 2 * D])
        qk = sb("qk", [TOK, TILES, 2 * D])
        vp = sb("vp", [TOK, TILES, 3, HEADS, HD + 1], BF16)
        vr = sb("vr", [TOK, 2, D])
        qta = sb("qta", [DA, 2, TOK])
        qtb = sb("qtb", [DB, 2, TOK])
        kbda = sb("kbda", [DA, 2, 8, TOK])
        kbdb = sb("kbdb", [DB, 2, 4, TOK])
        smax = sb("smax", [TOK, 2, HEADS])
        pth = sb("pth", [TOK, 2, HEADS, TOK], FP16)
        ptl = sb("ptl", [TOK, 2, HEADS, TOK], FP16)
        rsum = sb("rsum", [TOK, 2, HEADS])
        ao = sb("ao", [TOK, 2, D])
        aota = sb("aota", [DA, 2, TOK])
        aotb = sb("aotb", [DB, 2, TOK])
        hn2ta = sb("hn2ta", [DA, N])
        hn2tb = sb("hn2tb", [DB + 1, N])
        gmax = sb("gmax", [TOK, TILES, 8])
        gidx = sb("gidx", [TOK, TILES, 8], U32)
        gidxf = sb("gidxf", [TOK, TILES, 8])
        gneg = sb("gneg", [TOK, TILES])
        gexp = sb("gexp", [TOK, TILES, 8])
        gsum = sb("gsum", [TOK, TILES])
        grec = sb("grec", [TOK, TILES])
        gate = sb("gate", [TOK, TILES, 2])
        comb2 = sb("comb2", [TOK, TILES, 2, E])
        comb = sb("comb", [TOK, TILES, E])
        combt = sb("combt", [E, 2, TOK])
        with nc.sbuf_tensor("x_sb", [128, TILES, KC, TOK], F32) as x_sb, \
                nc.sbuf_tensor("sd", [TOK, 2, HEADS, TOK], F32) as sd, \
                nc.sbuf_tensor("probs", [TOK, 2, HEADS, TOK], F32) as pe_:
            pass
        ht = sb("ht", [128, 2, FC, N])

        ld_x = [sem(f"ld_x{t}") for t in range(TILES)]
        ld_embed = sem("ld_embed")
        ld_attn = sem("ld_attn")
        ld_const = sem("ld_const")
        ld_moe = sem("ld_moe")
        embed_done = sem("embed_done")
        h_copied = sem("h_copied")
        veps_ready = sem("veps_ready")
        r0_ready = sem("r0_ready")
        hn_ready = sem("hn_ready")
        hnt_done = sem("hnt_done")
        hnt_copied = sem("hnt_copied")
        qk_done = sem("qk_done")
        v_done = sem("v_done")
        rope_ready = sem("rope_ready")
        qk_ready = sem("qk_ready")
        v1_ready = sem("v1_ready")
        vr_ready = sem("vr_ready")
        v2_ready = sem("v2_ready")
        v3_ready = sem("v3_ready")
        ones_ready = sem("ones_ready")
        row_ready = sem("row_ready")
        qkt_done = sem("qkt_done")
        qt_copied = sem("qt_copied")
        kbd_ready = sem("kbd_ready")
        s_done = sem("s_done")
        sd_ready = sem("sd_ready")
        p_ready = sem("p_ready")
        pt_done = sem("pt_done")
        pth_ready = sem("pth_ready")
        ptl_ready = sem("ptl_ready")
        pv_done = sem("pv_done")
        ao_ready = sem("ao_ready")
        aot_done = sem("aot_done")
        aot_copied = sem("aot_copied")
        wo_done = sem("wo_done")
        h2_ready = sem("h2_ready")
        lg_done = sem("lg_done")
        gneg_ready = sem("gneg_ready")
        gexp_ready = sem("gexp_ready")
        comb_ready = sem("comb_ready")
        combt_done = sem("combt_done")
        combt_copied = sem("combt_copied")
        bias_done = sem("bias_done")
        l1_done = sem("l1_done")
        gelu_done = sem("gelu_done")
        l2_done = sem("l2_done")
        y_added = sem("y_added")
        dve_step = sem("dve_step")
        act_step = sem("act_step")
        stored = sem("stored")

        block = ctx.enter_context(nc.Block())

        @block.sync
        def _(sp):
            sp.dma_start(x_sb[:, 0], patches[0]).then_inc(ld_x[0], 16)
            sp.dma_start(wtok_sb[:, :, :], w_tok).then_inc(ld_embed, 16)
            sp.dma_start(tokrows_sb[:, :], tok_rows).then_inc(ld_embed, 16)
            sp.dma_start(toksel_sb[:, :], tok_sel).then_inc(ld_embed, 16)
            for t in range(1, TILES):
                sp.dma_start(x_sb[:, t], patches[t]).then_inc(ld_x[t], 16)
            sp.dma_start(ident_sb[:, :], ident).then_inc(ld_const, 16)
            sp.dma_start(identh_sb[:, :], ident_half).then_inc(ld_const, 16)
            for dst, src in ((wqkva_sb, w_qkv_a), (wqkvb_sb, w_qkv_b), (cos_sb, rope_cos), (sin_sb, rope_sin),
                             (mask_sb, mask), (headmask_sb, head_mask), (woa_sb, w_o_a), (wob_sb, w_o_b),
                             (wga_sb, w_g_a), (wgb_sb, w_g_b), (iota_sb, iota8)):
                sp.dma_start(dst[:, :], src).then_inc(ld_attn, 16)
            sp.dma_start(w1a_sb[:, :, :], w1_a).then_inc(ld_moe, 16)
            sp.dma_start(w1b_sb[:, :, :], w1_b).then_inc(ld_moe, 16)
            sp.dma_start(b1_sb[:, :], b1).then_inc(ld_moe, 16)
            sp.dma_start(w2_sb[:, :, :, :], w2).then_inc(ld_moe, 16)
            sp.dma_start(b2_sb[:, :], b2).then_inc(ld_moe, 16)
            for t in range(TILES):
                n = ROWS[t]
                sp.wait_ge(y_added, E * TILES - TILES + t + 1)
                sp.dma_start(out[t * TOK:t * TOK + n, :], h[0:n, t, :]).then_inc(stored, 16)
            sp.wait_ge(stored, 16 * TILES)

        ATTN_LOADS = 16 * 11

        @block.gpsimd
        def _(pool):
            nc.gpsimd.memset(vp[:, :, 0, :, HD:HD + 1], 1.0).then_inc(ones_ready, 1)
            for t in range(TILES):
                n = ROWS[t]
                pool.wait_ge(rope_ready, t + 1)
                nc.gpsimd.tensor_tensor(qk[0:n, t, :], ropec[0:n, t % 2, :], ropes[0:n, t % 2, :], ALU.add)\
                    .then_inc(qk_ready, 1)
                pool.wait_ge(v2_ready, t + 1)
                nc.gpsimd.tensor_tensor(vp[0:n, t, 2, :, 0:HD],
                                        vr[0:n, t % 2, :].rearrange("p (h d) -> p h d", d=HD),
                                        vp[0:n, t, 1, :, 0:HD], ALU.subtract).then_inc(v3_ready, 1)

        @block.tensor
        def _(pe):
            mm = nc.tensor.matmul
            tr = nc.tensor.transpose
            pe.wait_ge(ld_embed, 48)
            for t in range(TILES):
                n = ROWS[t]
                pe.wait_ge(ld_x[t], 16)
                for k in range(KC):
                    mm(bank[t][0:n, 0:D], x_sb[:, t, k, 0:n], wtok_sb[:, k, :], start=(k == 0), stop=False)
                mm(bank[t][0:n, 0:D], toksel_sb[:, t * TOK:t * TOK + n], tokrows_sb[:, :], start=False, stop=True)\
                    .then_inc(embed_done, 1)

            def turn(src, bk, n, t):
                tr(bk[0:DA, 0:n], src[0:n, t, 0:DA], ident_sb[0:n, 0:n])
                return tr(bk[0:DB, 128:128 + n], src[0:n, t, DA:D], ident_sb[0:n, 0:n])

            def normal_t(t):
                pe.wait_ge(hn_ready, t + 1)
                pe.wait_ge(h_copied, min(TILES, 5 + t))
                if t >= 2:
                    pe.wait_ge(hnt_copied, t - 1)
                turn(hn, bank[4 + t % 2], ROWS[t], t).then_inc(hnt_done, 1)

            def project(t):
                n, b = ROWS[t], t % 2
                pe.wait_ge(hnt_copied, t + 1)
                if t >= 2:
                    pe.wait_ge(rope_ready, t - 1)
                for j, (a, w) in enumerate(((hnta, wqkva_sb), (hntb, wqkvb_sb))):
                    last = mm(bank[6 + b][0:n, 0:2 * D], a[:, b, 0:n], w[:, 0:2 * D], start=(j == 0), stop=(j == 1))
                last.then_inc(qk_done, 1)
                if t >= 2:
                    pe.wait_ge(vr_ready, t - 1)
                    pe.wait_ge(v1_ready, t - 1)
                for j, (a, w) in enumerate(((hnta, wqkva_sb), (hntb, wqkvb_sb))):
                    last = mm(bank[2 + b][0:n, 0:D], a[:, b, 0:n], w[:, 2 * D:3 * D], start=(j == 0), stop=(j == 1))
                last.then_inc(v_done, 1)

            pe.wait_ge(ld_const, 32)
            pe.wait_ge(ld_attn, ATTN_LOADS)
            normal_t(0)
            for t in range(TILES):
                if t + 1 < TILES:
                    normal_t(t + 1)
                project(t)

            def qk_t(t):
                n = ROWS[t]
                pe.wait_ge(qk_ready, t + 1)
                if t == 0:
                    pe.wait_ge(rope_ready, TILES - 1)
                else:
                    pe.wait_ge(kbd_ready, t)
                    pe.wait_ge(qt_copied, t)
                for i, c in enumerate((0, D)):
                    tr(bank[6][0:DA, TOK * i:TOK * i + n], qk[0:n, t, c:c + DA], ident_sb[0:n, 0:n])
                    last = tr(bank[6][0:DB, TOK * (2 + i):TOK * (2 + i) + n], qk[0:n, t, c + DA:c + D],
                              ident_sb[0:n, 0:n])
                last.then_inc(qkt_done, 1)

            def scores(t):
                n, b = ROWS[t], t % 2
                pe.wait_ge(kbd_ready, t + 1)
                pe.wait_ge(qt_copied, t + 1)
                for g in range(GROUPS):
                    if t >= 1:
                        pe.wait_ge(sd_ready, GROUPS * (t - 1) + g + 1)
                    elif g == 2:
                        pe.wait_ge(vr_ready, TILES - 1)
                        pe.wait_ge(v1_ready, TILES - 1)
                    q, k = (qta[:, b, 0:n], kbda[:, b, HG * g:HG * g + HG, 0:n]) if g < 2 else \
                           (qtb[:, b, 0:n], kbdb[:, b, :, 0:n])
                    o = bank[g][0:n, 0:HG * TOK].rearrange("p (h s) -> p h s", s=TOK)[:, :, 0:n]
                    mm(o, q, k, start=True, stop=False)
                    mm(o, identh_sb[0:n, 0:n], mask_sb[0:n, 0:n].unsqueeze(1).to_broadcast([n, HG, n]),
                       start=False, stop=True).then_inc(s_done, 1)

            def probs_t(t):
                n, b = ROWS[t], t % 2
                for g in range(GROUPS):
                    i = GROUPS * t + g
                    pe.wait_ge(p_ready, i + 1)
                    if i >= 2:
                        pe.wait_ge(ptl_ready, i - 1)
                    elif i == 0:
                        pe.wait_ge(vr_ready, TILES)
                        pe.wait_ge(v1_ready, TILES)
                    for j in range(HG):
                        last = tr(bank[3 + i % 2][0:n, TOK * j:TOK * j + n], pe_[0:n, b, HG * g + j, 0:n],
                                  ident_sb[0:n, 0:n])
                    last.then_inc(pt_done, 1)

            def values(t):
                n, b = ROWS[t], t % 2
                pe.wait_ge(v3_ready, t + 1)
                if t == 0:
                    pe.wait_ge(ones_ready, 1)
                    pe.wait_ge(rope_ready, TILES)
                else:
                    pe.wait_ge(ao_ready, t)
                for hd in range(HEADS):
                    if hd % HG == 0:
                        pe.wait_ge(ptl_ready, GROUPS * t + hd // HG + 1)
                    c = hd * (HD + 1)
                    for i, (p, part) in enumerate(((pth, 0), (ptl, 0), (pth, 1), (ptl, 1), (pth, 2))):
                        w = HD + (part == 0)
                        last = mm(bank[7][0:n, c:c + w], p[0:n, b, hd, 0:n], vp[0:n, t, part, hd, 0:w],
                                  start=(i == 0), stop=(i == 4))
                last.then_inc(pv_done, 1)

            def attended_t(t):
                pe.wait_ge(ao_ready, t + 1)
                if t >= 1:
                    pe.wait_ge(h2_ready, t)
                b = t % 2
                n = ROWS[t]
                tr(bank[5][0:DA, 0:n], ao[0:n, b, 0:DA], ident_sb[0:n, 0:n])
                tr(bank[5][0:DB, 128:128 + n], ao[0:n, b, DA:D], ident_sb[0:n, 0:n]).then_inc(aot_done, 1)

            def out_project(t):
                n, b = ROWS[t], t % 2
                pe.wait_ge(aot_copied, t + 1)
                mm(bank[5][0:n, 256:256 + D], aota[:, b, 0:n], woa_sb[:, :], start=True, stop=False)
                mm(bank[5][0:n, 256:256 + D], aotb[:, b, 0:n], wob_sb[:, :], start=False, stop=True)\
                    .then_inc(wo_done, 1)

            qk_t(0)
            for i in range(TILES + 2):
                if i + 1 < TILES:
                    qk_t(i + 1)
                if i < TILES:
                    scores(i)
                if 2 <= i:
                    attended_t(i - 2)
                if 1 <= i <= TILES:
                    probs_t(i - 1)
                    values(i - 1)
                if 2 <= i:
                    out_project(i - 2)

            for t in range(TILES):
                n = ROWS[t]
                pe.wait_ge(hn_ready, TILES + t + 1)
                if t >= 2:
                    pe.wait_ge(hnt_copied, TILES + t - 1)
                turn(hn, bank[t % 2], n, t).then_inc(hnt_done, 1)
                pe.wait_ge(hnt_copied, TILES + t + 1)
                if t == 0:
                    pe.wait_ge(row_ready, 1)
                if t >= 2:
                    pe.wait_ge(comb_ready, t - 1)
                o = bank[2 + t % 2][0:n, 0:E]
                mm(o, hn2ta[:, t * TOK:t * TOK + n], wga_sb[:, :], start=True, stop=False)
                mm(o, hn2tb[:, t * TOK:t * TOK + n], wgb_sb[:, :], start=False, stop=True).then_inc(lg_done, 1)
            pe.wait_ge(ld_moe, 80)
            for t in range(TILES):
                n, b = ROWS[t], t % 2
                pe.wait_ge(comb_ready, t + 1)
                if t >= 2:
                    pe.wait_ge(combt_copied, t - 1)
                tr(bank[4 + b][0:E, 0:n], comb[0:n, t, :], ident_sb[0:n, 0:n]).then_inc(combt_done, 1)
                pe.wait_ge(combt_copied, t + 1)
                if t >= 2:
                    pe.wait_ge(h2_ready, TILES + t - 1)
                mm(bank[6 + b][0:n, 0:D], combt[:, b, 0:n], b2_sb[:, :], start=True, stop=True).then_inc(bias_done, 1)
            pe.wait_ge(h2_ready, 2 * TILES)

            for e in range(E):
                for half in range(2):
                    for f in range(FC):
                        i = (e * 2 + half) * FC + f
                        if i >= 4:
                            pe.wait_ge(gelu_done, i - 3)
                        o = bank[i % 4][:, 0:HALF]
                        cols = slice(half * HALF, half * HALF + HALF)
                        mm(o, w1a_sb[:, e, f * 128:f * 128 + 128], hn2ta[:, cols], start=True, stop=False)
                        mm(o, w1b_sb[:, e, f * 128:f * 128 + 128], hn2tb[0:DB, cols], start=False, stop=True)\
                            .then_inc(l1_done, 1)
                for t in range(TILES):
                    n = ROWS[t]
                    i = e * TILES + t
                    if t == 0:
                        pe.wait_ge(gelu_done, (e + 1) * 2 * FC)
                    if i >= 4:
                        pe.wait_ge(y_added, i - 3)
                    for f in range(FC):
                        last = mm(bank[4 + i % 4][0:n, 0:D], ht[:, e % 2, f, t * TOK:t * TOK + n], w2_sb[:, e, f, :],
                                  start=(f == 0), stop=(f == FC - 1))
                    last.then_inc(l2_done, 1)

        @block.scalar
        def _(act):
            fn = nc.scalar.activation
            steps = [0]

            def step(ins):
                steps[0] += 1
                ins.then_inc(act_step, 1)
                act.wait_ge(act_step, steps[0])

            def norm_root(t, rnd):
                n = ROWS[t]
                act.wait_ge(veps_ready, rnd * TILES + t + 1)
                step(fn(lnv[0:n, t:t + 1], veps[0:n, t:t + 1], ACT.Ln))
                fn(r0[0:n, t:t + 1], lnv[0:n, t:t + 1], ACT.Exp, scale=-0.5).then_inc(r0_ready, 1)

            def copy_normal_t(t, da, dbuf, rnd, bk):
                n = ROWS[t]
                act.wait_ge(hnt_done, rnd * TILES + t + 1)
                fn(da, bk[0:DA, 0:n], ACT.Copy)
                fn(dbuf, bk[0:DB, 128:128 + n], ACT.Copy).then_inc(hnt_copied, 1)

            for t in range(TILES + 1):
                if t < TILES:
                    n = ROWS[t]
                    act.wait_ge(embed_done, t + 1)
                    fn(h[0:n, t, :], bank[t][0:n, 0:D], ACT.Copy).then_inc(h_copied, 1)
                if t >= 1:
                    norm_root(t - 1, 0)

            def first_t(t):
                if t >= 2:
                    act.wait_ge(v_done, t - 1)
                copy_normal_t(t, hnta[:, t % 2, 0:ROWS[t]], hntb[:, t % 2, 0:ROWS[t]], 0, bank[4 + t % 2])

            def v_parts(t):
                n, b = ROWS[t], t % 2
                act.wait_ge(v_done, t + 1)
                fn(vp[0:n, t, 0, :, 0:HD], bank[2 + b][0:n, 0:D].rearrange("p (h d) -> p h d", d=HD), ACT.Copy)\
                    .then_inc(v1_ready, 1)
                act.wait_ge(vr_ready, t + 1)
                fn(vp[0:n, t, 1, :, 0:HD], vr[0:n, b, :].rearrange("p (h d) -> p h d", d=HD), ACT.Copy)\
                    .then_inc(v2_ready, 1)

            first_t(0)
            for t in range(TILES):
                if t + 1 < TILES:
                    first_t(t + 1)
                v_parts(t)

            def copy_q(t):
                n, b = ROWS[t], t % 2
                act.wait_ge(qkt_done, t + 1)
                if t >= 2:
                    act.wait_ge(s_done, GROUPS * (t - 1))
                fn(qta[:, b, 0:n], bank[6][0:DA, 0:n], ACT.Copy)
                fn(qtb[:, b, 0:n], bank[6][0:DB, 2 * TOK:2 * TOK + n], ACT.Copy).then_inc(qt_copied, 1)

            def exps(t, g):
                n, b = ROWS[t], t % 2
                act.wait_ge(sd_ready, GROUPS * t + g + 1)
                if t >= 2:
                    act.wait_ge(pt_done, GROUPS * (t - 2) + g + 1)
                fn(pe_[0:n, b, HG * g:HG * g + HG, 0:n], sd[0:n, b, HG * g:HG * g + HG, 0:n], ACT.Exp,
                   scale=float(HD) ** -0.5).then_inc(p_ready, 1)

            def high(t, g):
                n, b = ROWS[t], t % 2
                i = GROUPS * t + g
                act.wait_ge(pt_done, i + 1)
                if t >= 2:
                    act.wait_ge(pv_done, t - 1)
                fn(pth[0:n, b, HG * g:HG * g + HG, 0:n],
                   bank[3 + i % 2][0:n, 0:HG * TOK].rearrange("p (h s) -> p h s", s=TOK)[:, :, 0:n], ACT.Copy)\
                    .then_inc(pth_ready, 1)

            def copy_attended(t):
                n, b = ROWS[t], t % 2
                act.wait_ge(aot_done, t + 1)
                if t >= 2:
                    act.wait_ge(wo_done, t - 1)
                fn(aota[:, b, 0:n], bank[5][0:DA, 0:n], ACT.Copy)
                fn(aotb[:, b, 0:n], bank[5][0:DB, 128:128 + n], ACT.Copy).then_inc(aot_copied, 1)

            copy_q(0)
            for i in range(TILES + 2):
                if i + 1 < TILES:
                    copy_q(i + 1)
                if i >= 2:
                    copy_attended(i - 2)
                if i < TILES:
                    exps(i, 0)
                    exps(i, 1)
                if 1 <= i <= TILES:
                    high(i - 1, 0)
                if i < TILES:
                    exps(i, 2)
                if 1 <= i <= TILES:
                    high(i - 1, 1)
                    high(i - 1, 2)

            for t in range(TILES):
                norm_root(t, 1)
            for t in range(TILES + 1):
                if t < TILES:
                    n = ROWS[t]
                    c = slice(t * TOK, t * TOK + n)
                    copy_normal_t(t, hn2ta[:, c], hn2tb[0:DB, c], 1, bank[t % 2])
                if t >= 1:
                    n, u = ROWS[t - 1], t - 1
                    act.wait_ge(gneg_ready, t)
                    fn(gexp[0:n, u, :], gmax[0:n, u, :], ACT.Exp, bias=gneg[0:n, u:u + 1],
                       accum_out=gsum[0:n, u:u + 1]).then_inc(gexp_ready, 1)
            for t in range(TILES):
                n, b = ROWS[t], t % 2
                act.wait_ge(combt_done, t + 1)
                if t >= 2:
                    act.wait_ge(bias_done, t - 1)
                fn(combt[:, b, 0:n], bank[4 + b][0:E, 0:n], ACT.Copy).then_inc(combt_copied, 1)
            act.wait_ge(ld_moe, 80)
            for e in range(E):
                for half in range(2):
                    for f in range(FC):
                        i = (e * 2 + half) * FC + f
                        act.wait_ge(l1_done, i + 1)
                        if e >= 2 and half == 0 and f == 0:
                            act.wait_ge(l2_done, (e - 1) * TILES)
                        fn(ht[:, e % 2, f, half * HALF:half * HALF + HALF], bank[i % 4][:, 0:HALF], ACT.Gelu,
                           bias=b1_sb[:, e * FC + f:e * FC + f + 1]).then_inc(gelu_done, 1)

        @block.vector
        def _(dve):
            v = nc.vector
            steps = [0]

            def step(ins):
                steps[0] += 1
                ins.then_inc(dve_step, 1)
                dve.wait_ge(dve_step, steps[0])

            def norm_stats(t):
                n = ROWS[t]
                step(v.bn_stats(stats[0:n, t, :], h[0:n, t, :]))
                step(v.bn_aggr(mv[0:n, t, :], stats[0:n, t, :]))
                v.tensor_scalar(veps[0:n, t:t + 1], mv[0:n, t, 1:2], EPS, None, ALU.add).then_inc(veps_ready, 1)

            def norm_apply(t, rnd):
                n = ROWS[t]
                c = slice(t, t + 1)
                dve.wait_ge(r0_ready, rnd * TILES + t + 1)
                step(v.scalar_tensor_tensor(out=r1[0:n, c], in0=r0[0:n, c], scalar=veps[0:n, c], in1=r0[0:n, c],
                                            op0=ALU.mult, op1=ALU.mult))
                step(v.tensor_scalar(r2[0:n, c], r1[0:n, c], -0.5, 1.5, ALU.mult, ALU.add))
                step(v.tensor_tensor(rstd[0:n, c], r2[0:n, c], r0[0:n, c], ALU.mult))
                v.tensor_scalar(hn[0:n, t, :], h[0:n, t, :], mv[0:n, t, 0:1], rstd[0:n, c], ALU.subtract, ALU.mult)\
                    .then_inc(hn_ready, 1)

            v.memset(hn2tb[DB:DB + 1, :], 1.0).then_inc(row_ready, 1)
            for t in range(TILES + 1):
                if t < TILES:
                    dve.wait_ge(h_copied, t + 1)
                    norm_stats(t)
                if t >= 1:
                    norm_apply(t - 1, 0)

            dve.wait_ge(ld_attn, ATTN_LOADS)
            for t in range(TILES):
                n, b = ROWS[t], t % 2
                dve.wait_ge(qk_done, t + 1)
                if t >= 2:
                    dve.wait_ge(qk_ready, t - 1)
                x = bank[6 + b][0:n, 0:2 * D].rearrange("p (a c) -> p a c", a=2)
                v.tensor_tensor(ropec[0:n, b, :].rearrange("p (a c) -> p a c", a=2), x,
                                cos_sb[0:n, :].unsqueeze(1).to_broadcast([n, 2, D]), ALU.mult)
                x = bank[6 + b][0:n, 0:2 * D].rearrange("p (c s) -> p c s", s=2)
                y = ropes[0:n, b, :].rearrange("p (c s) -> p c s", s=2)
                sn = sin_sb[0:n, :].rearrange("p (c s) -> p c s", s=2)
                for a in range(2):
                    for s in range(2):
                        cs = slice(a * D // 2, (a + 1) * D // 2)
                        last = v.tensor_tensor(y[:, cs, s], x[:, cs, 1 - s], sn[:, :, s], ALU.mult)
                last.then_inc(rope_ready, 1)
                dve.wait_ge(v_done, t + 1)
                dve.wait_ge(v1_ready, t + 1)
                if t >= 2:
                    dve.wait_ge(v3_ready, t - 1)
                v.tensor_tensor(vr[0:n, b, :].rearrange("p (h d) -> p h d", d=HD),
                                bank[2 + b][0:n, 0:D].rearrange("p (h d) -> p h d", d=HD),
                                vp[0:n, t, 0, :, 0:HD], ALU.subtract).then_inc(vr_ready, 1)

            def spread_k(t):
                n, b = ROWS[t], t % 2
                dve.wait_ge(qkt_done, t + 1)
                dve.wait_ge(qt_copied, t + 1)
                if t >= 2:
                    dve.wait_ge(s_done, GROUPS * (t - 1))
                v.tensor_tensor(kbda[:, b, :, 0:n], bank[6][0:DA, TOK:TOK + n].unsqueeze(1).to_broadcast([DA, 8, n]),
                                headmask_sb[0:DA, :].unsqueeze(2).to_broadcast([DA, 8, n]), ALU.mult)
                v.tensor_tensor(kbdb[:, b, :, 0:n],
                                bank[6][0:DB, 3 * TOK:3 * TOK + n].unsqueeze(1).to_broadcast([DB, 4, n]),
                                headmask_sb[0:DB, 0:4].unsqueeze(2).to_broadcast([DB, 4, n]), ALU.mult)\
                    .then_inc(kbd_ready, 1)

            def less_max(t):
                n, b = ROWS[t], t % 2
                for g in range(GROUPS):
                    hs = slice(HG * g, HG * g + HG)
                    dve.wait_ge(s_done, GROUPS * t + g + 1)
                    if t >= 2:
                        dve.wait_ge(p_ready, GROUPS * (t - 2) + g + 1)
                    s = bank[g][0:n, 0:HG * TOK].rearrange("p (h s) -> p h s", s=TOK)[:, :, 0:n]
                    step(v.tensor_reduce(smax[0:n, b, hs], s, AX.X, ALU.max))
                    v.tensor_tensor(sd[0:n, b, hs, 0:n], s, smax[0:n, b, hs].unsqueeze(2).to_broadcast([n, HG, n]),
                                    ALU.subtract).then_inc(sd_ready, 1)

            def low(t):
                n, b = ROWS[t], t % 2
                for g in range(GROUPS):
                    i = GROUPS * t + g
                    hs = slice(HG * g, HG * g + HG)
                    dve.wait_ge(pth_ready, i + 1)
                    if t >= 2:
                        dve.wait_ge(pv_done, t - 1)
                    v.tensor_tensor(ptl[0:n, b, hs, 0:n],
                                    bank[3 + i % 2][0:n, 0:HG * TOK].rearrange("p (h s) -> p h s", s=TOK)[:, :, 0:n],
                                    pth[0:n, b, hs, 0:n], ALU.subtract).then_inc(ptl_ready, 1)

            def norm_out(t):
                n, b = ROWS[t], t % 2
                dve.wait_ge(pv_done, t + 1)
                if t >= 2:
                    dve.wait_ge(aot_done, t - 1)
                o = bank[7][0:n, 0:HEADS * (HD + 1)].rearrange("p (h d) -> p h d", d=HD + 1)
                step(v.reciprocal(rsum[0:n, b, :], o[:, :, HD]))
                v.tensor_tensor(ao[0:n, b, :].rearrange("p (h d) -> p h d", d=HD), o[:, :, 0:HD],
                                rsum[0:n, b, :].unsqueeze(2).to_broadcast([n, HEADS, HD]), ALU.mult)\
                    .then_inc(ao_ready, 1)

            def residual(t):
                n = ROWS[t]
                dve.wait_ge(wo_done, t + 1)
                v.tensor_tensor(h[0:n, t, :], bank[5][0:n, 256:256 + D], h[0:n, t, :], ALU.add).then_inc(h2_ready, 1)

            spread_k(0)
            for i in range(TILES + 2):
                if i + 1 < TILES:
                    spread_k(i + 1)
                if i < TILES:
                    less_max(i)
                if 1 <= i <= TILES:
                    low(i - 1)
                    norm_out(i - 1)
                if i >= 2:
                    residual(i - 2)
            dve.wait_ge(h2_ready, TILES)

            for t in range(TILES):
                norm_stats(t)
            for t in range(TILES):
                norm_apply(t, 1)
            for t in range(TILES):
                n = ROWS[t]
                lg = bank[2 + t % 2][0:n, 0:E]
                dve.wait_ge(lg_done, t + 1)
                step(v.max(gmax[0:n, t, :], lg))
                v.tensor_scalar(gneg[0:n, t:t + 1], gmax[0:n, t, 0:1], -1.0, None, ALU.mult).then_inc(gneg_ready, 1)
                step(v.max_index(gidx[0:n, t, :], gmax[0:n, t, :], lg))
                step(v.tensor_copy(gidxf[0:n, t, :], gidx[0:n, t, :]))
                dve.wait_ge(gexp_ready, t + 1)
                step(v.reciprocal(grec[0:n, t:t + 1], gsum[0:n, t:t + 1]))
                step(v.tensor_scalar(gate[0:n, t, :], gexp[0:n, t, 0:2], grec[0:n, t:t + 1], None, ALU.mult))
                for j in range(2):
                    last = v.tensor_scalar(comb2[0:n, t, j, :], iota_sb[0:n, :], gidxf[0:n, t, j:j + 1],
                                           gate[0:n, t, j:j + 1], ALU.is_equal, ALU.mult)
                step(last)
                v.tensor_tensor(comb[0:n, t, :], comb2[0:n, t, 0, :], comb2[0:n, t, 1, :], ALU.add)\
                    .then_inc(comb_ready, 1)
            for t in range(TILES):
                n = ROWS[t]
                dve.wait_ge(bias_done, t + 1)
                v.tensor_tensor(h[0:n, t, :], bank[6 + t % 2][0:n, 0:D], h[0:n, t, :], ALU.add).then_inc(h2_ready, 1)
            dve.wait_ge(h2_ready, 2 * TILES)
            for e in range(E):
                for t in range(TILES):
                    n = ROWS[t]
                    i = e * TILES + t
                    dve.wait_ge(l2_done, i + 1)
                    if e >= 1:
                        dve.wait_ge(y_added, i - TILES + 1)
                    v.scalar_tensor_tensor(out=h[0:n, t, :], in0=bank[4 + i % 4][0:n, 0:D],
                                           scalar=comb[0:n, t, e:e + 1], in1=h[0:n, t, :],
                                           op0=ALU.mult, op1=ALU.add).then_inc(y_added, 1)


def constants():
    import numpy as np
    bf16 = mybir.dt.np(BF16)
    i = np.arange(D // 2, dtype=np.float64)
    theta = 10000.0 ** (-2.0 * i / D)
    m_theta = np.repeat(np.arange(1, SEQ + 1, dtype=np.float64)[:, None] * theta[None, :], 2, axis=-1)
    pos = np.arange(TOK) % SEQ
    sign = np.where(np.arange(D) % 2 == 0, -1.0, 1.0)
    img = np.arange(TOK) // SEQ
    allowed = (img[:, None] == img[None, :]) & (pos[None, :] <= pos[:, None])
    tok = np.arange(N)
    return {
        "tok_sel": np.stack([tok % SEQ != 0, tok % SEQ == 0]).astype(np.float32),
        "rope_cos": np.cos(m_theta).astype(np.float32)[pos],
        "rope_sin": (np.sin(m_theta).astype(np.float32)[pos] * sign).astype(np.float32),
        "mask": np.where(allowed, 0.0, -1e30).astype(bf16),
        "ident": np.eye(128, dtype=np.float32),
        "ident_half": np.eye(128, dtype=np.float32).astype(bf16),
        "head_mask": (np.arange(128)[:, None] // HD == np.arange(8)[None, :]).astype(np.float32),
        "iota8": np.tile(np.arange(E, dtype=np.float32), (128, 1)),
    }


def laid_out(x, cls_tok, L0_tok_W, L0_tok_b, L0_attn_W_q, L0_attn_W_k, L0_attn_W_v, L0_attn_W_o, L0_ffn_Wg,
             L0_ffn_bg, L0_ffn_W1, L0_ffn_b1, L0_ffn_W2, L0_ffn_b2):
    import numpy as np
    a = [np.asarray(v) for v in (x, cls_tok, L0_tok_W, L0_tok_b, L0_attn_W_q, L0_attn_W_k, L0_attn_W_v, L0_attn_W_o,
                                 L0_ffn_Wg, L0_ffn_bg, L0_ffn_W1, L0_ffn_b1, L0_ffn_W2, L0_ffn_b2)]
    x, cls_tok, wt, bt, wq, wk, wv, wo, wg, bg, w1, b1, w2, b2 = a
    p = 16
    g = x.shape[2] // p
    cols = np.zeros((TILES * TOK, KC * 128), x.dtype).reshape(TILES * TOK, -1)
    body = x.reshape(IMAGES, 3, g, p, g, p).transpose(0, 2, 4, 1, 3, 5).reshape(IMAGES, g * g, -1)
    cols[:N].reshape(IMAGES, SEQ, -1)[:, 1:] = body
    wqkv = np.concatenate([wq.T, wk.T, wv.T], axis=1)
    return {
        "patches": cols.reshape(TILES, TOK, KC, 128).transpose(0, 3, 2, 1),
        "w_tok": wt.reshape(D, KC, 128).transpose(2, 1, 0),
        "tok_rows": np.stack([bt, cls_tok.reshape(D)]),
        "w_qkv_a": wqkv[:DA], "w_qkv_b": wqkv[DA:],
        "w_o_a": wo.T[:DA], "w_o_b": wo.T[DA:],
        "w_g_a": wg[:DA], "w_g_b": np.concatenate([wg[DA:], bg[None]]),
        "w1_a": w1[:, :DA].transpose(1, 0, 2), "w1_b": w1[:, DA:].transpose(1, 0, 2),
        "b1": b1.reshape(E * FC, 128).T,
        "w2": w2.reshape(E, FC, 128, D).transpose(2, 0, 1, 3),
        "b2": b2,
    }


_INS = ["patches", "w_tok", "tok_rows", "tok_sel", "w_qkv_a", "w_qkv_b", "rope_cos", "rope_sin", "mask", "ident",
        "ident_half", "head_mask", "w_o_a", "w_o_b", "w_g_a", "w_g_b", "iota8", "w1_a", "w1_b", "b1", "w2", "b2"]


def kernel(**inputs):
    import numpy as np
    import concourse.bacc as bacc
    from concourse.bass_utils import run_bass_kernel_spmd

    nc = bacc.Bacc("TRN2", target_bir_lowering=False, num_devices=1)
    given = {**constants(), **laid_out(**inputs)}
    arrays, args = {}, []
    for name in _INS:
        a = np.ascontiguousarray(given[name])
        arrays[f"in_{name}"] = a
        args.append(nc.dram_tensor(f"in_{name}", a.shape, mybir.dt.from_np(a.dtype), kind="ExternalInput").ap())
    out = nc.dram_tensor("out_y", (N, D), F32, kind="ExternalOutput").ap()
    vit_block(nc, *args, out)
    r = run_bass_kernel_spmd(nc, [arrays], core_ids=[0])
    return r.results[0]["out_y"].reshape(IMAGES, SEQ, D)
```

```python
import concourse.bass as bass
from concourse import mybir
from contextlib import ExitStack

F32 = mybir.dt.float32
BF16 = mybir.dt.bfloat16
FP16 = mybir.dt.float16
F32R = mybir.dt.float32r
I32 = mybir.dt.int32
U32 = mybir.dt.uint32
ALU = mybir.AluOpType
ACT = mybir.ActivationFunctionType
AX = mybir.AxisListType

IMAGES = 16
SEQ = 37
GROUP = 3
TOK = GROUP * SEQ
N = IMAGES * SEQ
TILES = -(-N // TOK)
ROWS = [min(TOK, N - t * TOK) for t in range(TILES)]
D = 192
DA, DB = 128, D - 128
HEADS, HD = 12, 16
HG = 4
GROUPS = HEADS // HG
KC = 6
E = 8
F = 768
FC = F // 128
EPS = 1e-5

BLK = 128
CAP = -(-N // BLK) * BLK
MAXB = CAP // BLK
SPARE = E * CAP
NB = (2 * N - E) // BLK + E
C_TOK, C_IDX, C_GATE, PAY = 256, 257, 259, 261
A_HI, A_LO, B_HI, B_LO, W2_HL = 0, F, 2 * F, 3 * F, 4 * F
WCOLS = 4 * F + FC * 2 * D
EARLY = 6
VC = 3 * HD + 1
G0, G1, LG, CT = 0, TOK, 2 * TOK, 256
PC = 2 * HD + 1
FH = F // 2
LAG = 3
T_EXP, T_ROW, T_COLS = 0, NB, 2 * NB


class Region:

    def __init__(self, nc, at, end):
        self.nc, self.at, self.end = nc, at, end

    def __call__(self, name, shape, dt=F32):
        size = mybir.dt.size(dt)
        for n in shape[1:]:
            size *= n
        t = self.nc.alloc_sbuf_tensor_at(name, shape, dt, offset=self.at)
        self.at += -(-size // 32) * 32
        assert self.at <= self.end, (name, self.at, self.end)
        return t


def vit_block(nc, patches, w_tok, tok_rows, tok_sel, w_qkv_a, w_qkv_b, rope_cos, rope_sin, mask,
              ident, ident_half, head_mask, w_o_a, w_o_b, w_g_a, w_g_b, iota8, w1_a, w1_bb, w1_b, b1, w2, b2,
              before, ones_half, tok_ids, pad_rows, row_base, block_steps, lower8, block_ids, out):
    xs = nc.dram_tensor("dispatched", (SPARE + BLK, PAY), F32, kind="Internal").ap()
    ctx = ExitStack()
    with ctx:
        def sem(name):
            return ctx.enter_context(nc.semaphore(name))

        bank = [ctx.enter_context(nc.psum_tensor(f"bank{i}", [128, 512], F32)) for i in range(8)]
        slab = ctx.enter_context(nc.sbuf_tensor("slab", [128, (nc.sbuf_bytes_remaining - 64) // 4], F32))
        start = -(-(nc.sbuf_base - slab.shape[1] * 4) // 32) * 32
        top = nc.sbuf_base

        keep = Region(nc, start, top)
        ident_sb = keep("ident_sb", [128, 128])
        identh_sb = keep("identh_sb", [128, 128], BF16)
        headmask_sb = keep("headmask_sb", [128, 8])
        woa_sb = keep("woa_sb", [DA, D])
        wob_sb = keep("wob_sb", [DB, D])
        wga_sb = keep("wga_sb", [DA, E])
        wgb_sb = keep("wgb_sb", [DB + 1, E])
        iota_sb = keep("iota_sb", [128, E])
        b2_sb = keep("b2_sb", [E, D])
        before_sb = keep("before_sb", [TOK, TOK], BF16)
        onesh_sb = keep("onesh_sb", [TOK, 128], BF16)
        tokids_sb = keep("tokids_sb", [TOK, TILES], U32)
        rowbase_sb = keep("rowbase_sb", [128, E])
        steps_sb = keep("steps_sb", [128, MAXB])
        lower8_sb = keep("lower8_sb", [128, E, E])
        blockids_sb = keep("blockids_sb", [128, NB])
        b1lo_sb = keep("b1lo_sb", [E, F], F32R)
        h = keep("h", [TOK, TILES, D])
        stats = keep("stats", [TOK, TILES, 6])
        mv = keep("mv", [TOK, TILES, 2])
        veps = keep("veps", [TOK, TILES])
        rstd = keep("rstd", [TOK, TILES])
        nhalf = keep("nhalf", [128, 1])
        ao = keep("ao", [TOK, 2, D])
        aota = keep("aota", [DA, 2, TOK])
        aotb = keep("aotb", [DB, 2, TOK])
        smax = keep("smax", [TOK, 2, HEADS])
        sneg = keep("sneg", [TOK, 2, HEADS])
        rsum = keep("rsum", [TOK, 2, HEADS])
        hn2ta = keep("hn2ta", [DA, 2, TOK])
        hn2tb = keep("hn2tb", [DB + 1, 2, TOK])
        combt = keep("combt", [E, 2, TOK])
        pay = keep("pay", [TOK, 3, PAY])
        gmax = keep("gmax", [TOK, TILES, 8])
        gidx = keep("gidx", [TOK, TILES, 8], U32)
        gneg = keep("gneg", [TOK, TILES])
        gexp = keep("gexp", [TOK, TILES, 8])
        gsum = keep("gsum", [TOK, TILES])
        grec = keep("grec", [TOK, TILES])
        chosen = keep("chosen", [TOK, TILES, 2, E])
        member = keep("member", [TOK, TILES, E], BF16)
        comb2 = keep("comb2", [TOK, 2, 2, E])
        comb = keep("comb", [TOK, TILES, E])
        rowof = keep("rowof", [TOK, TILES, E])
        rowsel = keep("rowsel", [TOK, 2, 2, E])
        rowf = keep("rowf", [TOK, TILES, 2])
        rowu = keep("rowu", [TOK, TILES, 2], U32)
        blocks = keep("blocks", [128, E])
        ends = keep("ends", [128, E])
        table = keep("table", [128, NB])
        tablei = keep("tablei", [128, T_COLS], I32)

        w_at = keep.at
        we = Region(nc, w_at, top)("we", [128, E, WCOLS], F32R)
        raw = [Region(nc, w_at + e * WCOLS * 4, top)(f"raw{e}", [128, WCOLS], F32) for e in range(E)]
        moe = Region(nc, w_at + E * WCOLS * 4, top)
        xin = moe("xin", [BLK, 2, PAY])
        xahi = moe("xahi", [DA, BLK], F32R)
        xalo = moe("xalo", [DA, BLK], F32R)
        xb1 = moe("xb1", [128, BLK], F32R)
        xb2 = moe("xb2", [DB + 2, BLK], F32R)
        scratch = Region(nc, moe.at, top)
        over = scratch("over", [128, E, MAXB])
        blocks8 = scratch("blocks8", [128, E, E])
        passed = scratch("passed", [128, 2, NB, E])
        rest = scratch("rest", [128, E])
        tmp_nb = scratch("tmp_nb", [128, 2, NB])
        hid = moe("hid", [BLK, F])
        hthi = moe("hthi", [128, FC, BLK], F32R)
        htlo = moe("htlo", [128, FC, BLK], F32R)
        y1 = moe("y1", [BLK, D])
        y = moe("y", [BLK, 2, D])
        gsel = moe("gsel", [BLK, 2, 2])
        gblk = moe("gblk", [BLK, NB])
        tokblk = moe("tokblk", [BLK, NB], U32)

        early = Region(nc, w_at + EARLY * WCOLS * 4, top)
        wqkva_sb = early("wqkva_sb", [DA, 3 * D])
        wqkvb_sb = early("wqkvb_sb", [DB, 3 * D])
        cos_sb = early("cos_sb", [TOK, D])
        sin_sb = early("sin_sb", [TOK, D])
        mask_sb = early("mask_sb", [TOK, TOK], BF16)
        qk = early("qk", [TOK, TILES, 2 * D])
        vp = early("vp", [TOK, TILES, HEADS, VC], BF16)
        qta = early("qta", [DA, 2, TOK])
        qtb = early("qtb", [DB, 2, TOK])
        first = Region(nc, early.at, top)
        x_sb = first("x_sb", [128, TILES, KC, TOK])
        wtok_sb = first("wtok_sb", [128, KC, D])
        tokrows_sb = first("tokrows_sb", [2, D])
        toksel_sb = first("toksel_sb", [2, N])
        b1raw_sb = first("b1raw_sb", [E, F])
        b1hi_sb = first("b1hi_sb", [E, F], F32R)
        second = Region(nc, early.at, top)
        probs = second("probs", [TOK, 2, HEADS, TOK])
        pth = second("pth", [TOK, 2, HEADS, TOK], FP16)
        ptl = second("ptl", [TOK, 2, HEADS, TOK], FP16)
        third = Region(nc, first.at, top)
        hn = third("hn", [TOK, TILES, D])
        project = Region(nc, early.at, first.at)
        hnta = project("hnta", [DA, 2, TOK])
        hntb = project("hntb", [DB, 2, TOK])
        ropec = project("ropec", [TOK, 2, 2 * D])
        ropes = project("ropes", [TOK, 2, 2 * D])
        vr = project("vr", [TOK, 2, D])
        fourth = Region(nc, second.at, third.at)
        kbda = fourth("kbda", [DA, 2, 8, TOK])
        kbdb = fourth("kbdb", [DB, 2, 4, TOK])

        ld_x = [sem(f"ld_x{t}") for t in range(TILES)]
        ld_embed = sem("ld_embed")
        ld_attn = sem("ld_attn")
        ld_const = sem("ld_const")
        ld_rest = sem("ld_rest")
        embed_done = sem("embed_done")
        h_copied = sem("h_copied")
        veps_ready = sem("veps_ready")
        rstd_ready = sem("rstd_ready")
        hn_ready = sem("hn_ready")
        hnt_done = sem("hnt_done")
        hnt_copied = sem("hnt_copied")
        qk_done = sem("qk_done")
        v_done = sem("v_done")
        rope_ready = sem("rope_ready")
        qk_ready = sem("qk_ready")
        v1_ready = sem("v1_ready")
        vr_ready = sem("vr_ready")
        v2_ready = sem("v2_ready")
        v3_ready = sem("v3_ready")
        ones_ready = sem("ones_ready")
        qkt_done = sem("qkt_done")
        qt_copied = sem("qt_copied")
        kbd_ready = sem("kbd_ready")
        s_done = sem("s_done")
        max_ready = sem("max_ready")
        p_ready = sem("p_ready")
        pt_done = sem("pt_done")
        pth_ready = sem("pth_ready")
        ptl_ready = sem("ptl_ready")
        pv_done = sem("pv_done")
        ao_ready = sem("ao_ready")
        aot_done = sem("aot_done")
        aot_copied = sem("aot_copied")
        wo_done = sem("wo_done")
        h2_ready = sem("h2_ready")
        h3_ready = sem("h3_ready")
        lg_done = sem("lg_done")
        gneg_ready = sem("gneg_ready")
        gexp_ready = sem("gexp_ready")
        comb_ready = sem("comb_ready")
        combt_done = sem("combt_done")
        combt_copied = sem("combt_copied")
        bias_done = sem("bias_done")
        chosen_ready = sem("chosen_ready")
        rank_done = sem("rank_done")
        row_ready = sem("row_ready")
        scattered = [sem(f"scattered{b}") for b in range(3)]
        out_first = sem("out_first")
        count_done = sem("count_done")
        table_ready = sem("table_ready")
        padded = sem("padded")
        hi_ready = sem("hi_ready")
        w_raw = [sem(f"w_raw{e}") for e in range(E)]
        b1_raw = sem("b1_raw")
        b1_lo = sem("b1_lo")
        b1_rows = sem("b1_rows")
        lo_dve = sem("lo_dve")
        lo_pool = sem("lo_pool")
        early_free = sem("early_free")
        xin_ld = [sem(f"xin_ld{b}") for b in range(2)]
        xt_done = sem("xt_done")
        xhi_ready = sem("xhi_ready")
        xlo_ready = sem("xlo_ready")
        gate_ready = sem("gate_ready")
        l1_done = sem("l1_done")
        gelu_done = sem("gelu_done")
        ht_done = sem("ht_done")
        hthi_ready = sem("hthi_ready")
        htlo_ready = sem("htlo_ready")
        l2_done = sem("l2_done")
        y1_ready = sem("y1_ready")
        y_ready = sem("y_ready")
        added = sem("added")
        fixed = sem("fixed")
        dve_step = sem("dve_step")

        ATTN_LOADS = 16 * 4
        REST_LOADS = 16 * 15

        block = ctx.enter_context(nc.Block())

        @block.sync
        def _(sp):
            sp.dma_start(x_sb[:, 0], patches[0]).then_inc(ld_x[0], 16)
            sp.dma_start(wtok_sb[:, :, :], w_tok).then_inc(ld_embed, 16)
            sp.dma_start(tokrows_sb[:, :], tok_rows).then_inc(ld_embed, 16)
            sp.dma_start(toksel_sb[:, :], tok_sel).then_inc(ld_embed, 16)
            for t in range(1, TILES):
                sp.dma_start(x_sb[:, t], patches[t]).then_inc(ld_x[t], 16)
            sp.dma_start(ident_sb[:, :], ident).then_inc(ld_const, 16)
            sp.dma_start(identh_sb[:, :], ident_half).then_inc(ld_const, 16)
            for dst, src in ((wqkva_sb, w_qkv_a), (wqkvb_sb, w_qkv_b), (cos_sb, rope_cos), (sin_sb, rope_sin)):
                sp.dma_start(dst[:, :], src).then_inc(ld_attn, 16)
            for dst, src in ((mask_sb, mask), (headmask_sb, head_mask), (woa_sb, w_o_a), (wob_sb, w_o_b),
                             (wga_sb, w_g_a), (wgb_sb, w_g_b), (iota_sb, iota8), (before_sb, before),
                             (onesh_sb, ones_half), (tokids_sb, tok_ids), (rowbase_sb, row_base),
                             (steps_sb, block_steps), (lower8_sb, lower8), (blockids_sb, block_ids), (b2_sb, b2)):
                sp.dma_start(dst[:], src).then_inc(ld_rest, 16)
            sp.dma_start(b1raw_sb[:, :], b1).then_inc(b1_raw, 16)

            def load_raw(e):
                sp.dma_start(raw[e][:, A_LO:A_LO + F], w1_a[:, e, :]).then_inc(w_raw[e], 16)
                sp.dma_start(raw[e][0:DB, B_LO:B_LO + F], w1_b[:, e, :]).then_inc(w_raw[e], 16)
                sp.dma_start(raw[e][:, B_HI:B_HI + F], w1_bb[:, e, :]).then_inc(w_raw[e], 16)
                sp.dma_start(raw[e][:, W2_HL:WCOLS].rearrange("p (f c) -> p f c", c=2 * D)[:, :, D:2 * D],
                             w2[:, e, :, :]).then_inc(w_raw[e], 16)

            for e in range(EARLY):
                load_raw(e)
            sp.dma_start(xs.rearrange("(a p) c -> a p c", p=BLK),
                         pad_rows.unsqueeze(0).to_broadcast([(SPARE + BLK) // BLK, BLK, PAY])).then_inc(padded, 16)
            sp.dma_start(out[N:N + BLK, :], pad_rows[:, 0:D]).then_inc(out_first, 16)
            sp.wait_ge(early_free, 1)
            for e in range(EARLY, E):
                load_raw(e)
            for t in range(TILES):
                n = ROWS[t]
                sp.wait_ge(h3_ready, t + 1)
                sp.dma_start(out[t * TOK:t * TOK + n, :], h[0:n, t, :]).then_inc(out_first, 16)
            sp.wait_ge(table_ready, 1)
            for b in range(3):
                sp.wait_ge(scattered[b], 32 * (TILES // 3))
            for b in range(NB):
                row = sp.value_load(tablei[0:1, T_ROW + b:T_ROW + b + 1], min_val=0, max_val=SPARE)
                if b >= 2:
                    sp.wait_ge(xt_done, b - 1)
                    sp.wait_ge(gate_ready, b - 1)
                sp.dma_start(xin[:, b % 2, :], xs[bass.ds(row, BLK), :]).then_inc(xin_ld[b % 2], 16)

        @block.gpsimd
        def _(pool):
            def root(t, rnd):
                n = ROWS[t]
                pool.wait_ge(veps_ready, rnd * TILES + t + 1)
                nc.gpsimd.tensor_tensor(rstd[0:n, t:t + 1], veps[0:n, t:t + 1], nhalf[0:n, :], ALU.pow)\
                    .then_inc(rstd_ready, 1)

            def split_w2(e):
                pool.wait_ge(hi_ready, 2 * e + 2)
                hl = we[:, e, W2_HL:WCOLS].rearrange("p (f c) -> p f c", c=2 * D)
                whole = raw[e][:, W2_HL:WCOLS].rearrange("p (f c) -> p f c", c=2 * D)
                nc.gpsimd.tensor_tensor(hl[:, :, D:2 * D], whole[:, :, D:2 * D], hl[:, :, 0:D], ALU.subtract)\
                    .then_inc(lo_pool, 1)

            def split_w1(e):
                pool.wait_ge(hi_ready, 2 * e + 1)
                nc.gpsimd.tensor_tensor(we[:, e, A_LO:A_LO + F], raw[e][:, A_LO:A_LO + F], we[:, e, A_HI:A_HI + F],
                                        ALU.subtract)
                nc.gpsimd.tensor_tensor(we[0:DB, e, B_LO:B_LO + F], raw[e][0:DB, B_LO:B_LO + F],
                                        we[0:DB, e, B_HI:B_HI + F], ALU.subtract).then_inc(lo_pool, 1)

            def bias_rows(e0, e1):
                pool.dma_start(we[DB:DB + 1, e0:e1, B_LO:B_LO + F], b1[e0:e1, :]).then_inc(b1_rows, 16)
                pool.dma_start(we[DB + 1:DB + 2, e0:e1, B_LO:B_LO + F], b1lo_sb[e0:e1, :]).then_inc(b1_rows, 16)

            def dispatch(t):
                n = ROWS[t]
                pool.wait_ge(row_ready, t + 1)
                if t == 0:
                    pool.wait_ge(padded, 16)
                for j in range(2):
                    pool.indirect_dma_start(xs, bass.IndirectOffsetOnAxis(ap=rowu[0:n, t, j:j + 1], axis=0),
                                            pay[0:n, t % 3, :], None).then_inc(scattered[t % 3], 16)

            pool.wait_ge(fixed, 1)
            nc.gpsimd.memset(vp[:, :, :, HD:HD + 1], 1.0).then_inc(ones_ready, 1)
            for t in range(TILES):
                root(t, 0)
            for t in range(TILES):
                n = ROWS[t]
                pool.wait_ge(rope_ready, t + 1)
                nc.gpsimd.tensor_tensor(qk[0:n, t, :], ropec[0:n, t % 2, :], ropes[0:n, t % 2, :], ALU.add)\
                    .then_inc(qk_ready, 1)
                pool.wait_ge(v2_ready, t + 1)
                nc.gpsimd.tensor_tensor(vp[0:n, t, :, PC:VC],
                                        vr[0:n, t % 2, :].rearrange("p (h d) -> p h d", d=HD),
                                        vp[0:n, t, :, HD + 1:PC], ALU.subtract).then_inc(v3_ready, 1)
            pool.wait_ge(b1_lo, 1)
            bias_rows(0, EARLY)
            for i in range(TILES + LAG + 1):
                if LAG <= i < TILES + LAG:
                    root(i - LAG, 1)
                if i == TILES:
                    pool.wait_ge(early_free, 1)
                    bias_rows(EARLY, E)
                if i < EARLY:
                    split_w1(i)
                    split_w2(i)
                if i >= LAG + 1:
                    dispatch(i - LAG - 1)
            for e in range(EARLY, E):
                split_w2(e)
            pool.wait_ge(out_first, 16 * (TILES + 1))
            for b in range(NB):
                pool.wait_ge(y_ready, b + 1)
                pool.wait_ge(gate_ready, b + 1)
                if b >= 1:
                    pool.wait_ge(added, 16 * b)
                pool.indirect_dma_start(out, bass.IndirectOffsetOnAxis(ap=tokblk[:, b:b + 1], axis=0),
                                        y[:, b % 2, :], None, compute_op=ALU.add).then_inc(added, 16)
            pool.wait_ge(added, 16 * NB)

        @block.tensor
        def _(pe):
            mm = nc.tensor.matmul
            tr = nc.tensor.transpose
            pe.wait_ge(ld_embed, 48)
            for t in range(TILES):
                n = ROWS[t]
                pe.wait_ge(ld_x[t], 16)
                for k in range(KC):
                    mm(bank[t][0:n, 0:D], x_sb[:, t, k, 0:n], wtok_sb[:, k, :], start=(k == 0), stop=False)
                mm(bank[t][0:n, 0:D], toksel_sb[:, t * TOK:t * TOK + n], tokrows_sb[:, :], start=False, stop=True)\
                    .then_inc(embed_done, 1)

            def turn(src, bk, n, t):
                tr(bk[0:DA, 0:n], src[0:n, t, 0:DA], ident_sb[0:n, 0:n])
                return tr(bk[0:DB, 128:128 + n], src[0:n, t, DA:D], ident_sb[0:n, 0:n])

            def normal_t(t):
                pe.wait_ge(hn_ready, t + 1)
                pe.wait_ge(h_copied, min(TILES, 5 + t))
                if t >= 2:
                    pe.wait_ge(hnt_copied, t - 1)
                turn(hn, bank[4 + t % 2], ROWS[t], t).then_inc(hnt_done, 1)

            def project(t):
                n, b = ROWS[t], t % 2
                pe.wait_ge(hnt_copied, t + 1)
                if t >= 2:
                    pe.wait_ge(rope_ready, t - 1)
                for j, (a, w) in enumerate(((hnta, wqkva_sb), (hntb, wqkvb_sb))):
                    last = mm(bank[6 + b][0:n, 0:2 * D], a[:, b, 0:n], w[:, 0:2 * D], start=(j == 0), stop=(j == 1))
                last.then_inc(qk_done, 1)
                if t >= 2:
                    pe.wait_ge(vr_ready, t - 1)
                    pe.wait_ge(v1_ready, t - 1)
                for j, (a, w) in enumerate(((hnta, wqkva_sb), (hntb, wqkvb_sb))):
                    last = mm(bank[2 + b][0:n, 0:D], a[:, b, 0:n], w[:, 2 * D:3 * D], start=(j == 0), stop=(j == 1))
                last.then_inc(v_done, 1)

            pe.wait_ge(ld_const, 32)
            pe.wait_ge(ld_attn, ATTN_LOADS)
            normal_t(0)
            for t in range(TILES):
                if t + 1 < TILES:
                    normal_t(t + 1)
                project(t)

            def qk_t(t):
                n = ROWS[t]
                pe.wait_ge(qk_ready, t + 1)
                if t == 0:
                    pe.wait_ge(rope_ready, TILES - 1)
                else:
                    pe.wait_ge(kbd_ready, t)
                    pe.wait_ge(qt_copied, t)
                for i, c in enumerate((0, D)):
                    tr(bank[6][0:DA, TOK * i:TOK * i + n], qk[0:n, t, c:c + DA], ident_sb[0:n, 0:n])
                    last = tr(bank[6][0:DB, TOK * (2 + i):TOK * (2 + i) + n], qk[0:n, t, c + DA:c + D],
                              ident_sb[0:n, 0:n])
                last.then_inc(qkt_done, 1)

            def scores(t, groups):
                n, b = ROWS[t], t % 2
                pe.wait_ge(kbd_ready, t + 1)
                pe.wait_ge(qt_copied, t + 1)
                for g in groups:
                    if t >= 1:
                        pe.wait_ge(p_ready, GROUPS * (t - 1) + g + 1)
                    elif g == 2:
                        pe.wait_ge(vr_ready, TILES - 1)
                        pe.wait_ge(v1_ready, TILES - 1)
                    q, k = (qta[:, b, 0:n], kbda[:, b, HG * g:HG * g + HG, 0:n]) if g < 2 else \
                           (qtb[:, b, 0:n], kbdb[:, b, :, 0:n])
                    o = bank[g][0:n, 0:HG * TOK].rearrange("p (h s) -> p h s", s=TOK)[:, :, 0:n]
                    mm(o, q, k, start=True, stop=False)
                    mm(o, identh_sb[0:n, 0:n], mask_sb[0:n, 0:n].unsqueeze(1).to_broadcast([n, HG, n]),
                       start=False, stop=True).then_inc(s_done, 1)

            def probs_t(t, groups):
                n, b = ROWS[t], t % 2
                for g in groups:
                    i = GROUPS * t + g
                    pe.wait_ge(p_ready, i + 1)
                    if i >= 2:
                        pe.wait_ge(ptl_ready, i - 1)
                    elif i == 0:
                        pe.wait_ge(vr_ready, TILES)
                        pe.wait_ge(v1_ready, TILES)
                    for j in range(HG):
                        last = tr(bank[3 + i % 2][0:n, TOK * j:TOK * j + n], probs[0:n, b, HG * g + j, 0:n],
                                  ident_sb[0:n, 0:n])
                    last.then_inc(pt_done, 1)

            def values(t):
                n, b = ROWS[t], t % 2
                pe.wait_ge(v3_ready, t + 1)
                if t == 0:
                    pe.wait_ge(ones_ready, 1)
                    pe.wait_ge(rope_ready, TILES)
                else:
                    pe.wait_ge(h2_ready, t)
                for hd in range(HEADS):
                    if hd % HG == 0:
                        pe.wait_ge(ptl_ready, GROUPS * t + hd // HG + 1)
                    c = hd * PC
                    mm(bank[7][0:n, c:c + PC], pth[0:n, b, hd, 0:n], vp[0:n, t, hd, 0:PC], start=True, stop=False)
                    mm(bank[7][0:n, c:c + HD], pth[0:n, b, hd, 0:n], vp[0:n, t, hd, PC:VC], start=False, stop=False)
                    last = mm(bank[7][0:n, c:c + PC], ptl[0:n, b, hd, 0:n], vp[0:n, t, hd, 0:PC], start=False, stop=True)
                last.then_inc(pv_done, 1)

            def attended_t(t):
                pe.wait_ge(ao_ready, t + 1)
                b = t % 2
                n = ROWS[t]
                tr(bank[7][0:DA, 0:n], ao[0:n, b, 0:DA], ident_sb[0:n, 0:n])
                tr(bank[7][0:DB, TOK:TOK + n], ao[0:n, b, DA:D], ident_sb[0:n, 0:n]).then_inc(aot_done, 1)

            def out_project(t):
                n, b = ROWS[t], t % 2
                pe.wait_ge(aot_copied, t + 1)
                mm(bank[7][0:n, 2 * TOK:2 * TOK + D], aota[:, b, 0:n], woa_sb[:, :], start=True, stop=False)
                mm(bank[7][0:n, 2 * TOK:2 * TOK + D], aotb[:, b, 0:n], wob_sb[:, :], start=False, stop=True).then_inc(wo_done, 1)

            def gates_t(t):
                n = ROWS[t]
                pe.wait_ge(hn_ready, TILES + t + 1)
                if t >= 1:
                    pe.wait_ge(h3_ready, t)
                tr(bank[5][0:DA, G0:G0 + n], pay[0:n, t % 3, 0:DA], ident_sb[0:n, 0:n])
                tr(bank[5][0:DB, G1:G1 + n], pay[0:n, t % 3, DA:D], ident_sb[0:n, 0:n]).then_inc(hnt_done, 1)

            def logits(t):
                n, b = ROWS[t], t % 2
                pe.wait_ge(hnt_copied, TILES + t + 1)
                mm(bank[5][0:n, LG:LG + E], hn2ta[:, b, 0:n], wga_sb[:, :], start=True, stop=False)
                mm(bank[5][0:n, LG:LG + E], hn2tb[:, b, 0:n], wgb_sb[:, :], start=False, stop=True).then_inc(lg_done, 1)

            def gates_back(t):
                n = ROWS[t]
                pe.wait_ge(comb_ready, t + 1)
                tr(bank[5][0:E, CT:CT + n], comb[0:n, t, :], ident_sb[0:n, 0:n]).then_inc(combt_done, 1)

            def ranks(t):
                n = ROWS[t]
                pe.wait_ge(chosen_ready, t + 1)
                pe.wait_ge(combt_copied, t + 1)
                o = bank[5][0:n, LG:LG + E]
                last = mm(o, before_sb[0:n, 0:n], member[0:n, t, :], start=True, stop=(t == 0))
                for u in range(t):
                    last = mm(o, onesh_sb[0:ROWS[u], 0:n], member[0:ROWS[u], u, :], start=False, stop=(u == t - 1))
                last.then_inc(rank_done, 1)

            def bias2(t):
                n, b = ROWS[t], t % 2
                pe.wait_ge(row_ready, t + 1)
                mm(bank[5][0:n, 0:D], combt[:, b, 0:n], b2_sb[:, :], start=True, stop=True).then_inc(bias_done, 1)

            pe.wait_ge(ld_rest, REST_LOADS)
            qk_t(0)
            for i in range(TILES + LAG + 1):
                if 1 <= i <= TILES:
                    probs_t(i - 1, (0, 1))
                if 2 <= i < TILES + 2:
                    attended_t(i - 2)
                if i + 1 < TILES:
                    qk_t(i + 1)
                if i >= LAG + 1:
                    ranks(i - LAG - 1)
                if i < TILES:
                    scores(i, (0, 1))
                if 1 <= i <= TILES:
                    probs_t(i - 1, (2,))
                if i == TILES + LAG:
                    for t in range(TILES):
                        last = mm(bank[0][:, 0:E], onesh_sb[0:ROWS[t], :], member[0:ROWS[t], t, :],
                                  start=(t == 0), stop=(t == TILES - 1))
                    last.then_inc(count_done, 1)
                if i >= LAG + 1:
                    bias2(i - LAG - 1)
                if 2 <= i < TILES + 2:
                    out_project(i - 2)
                if i < TILES:
                    scores(i, (2,))
                if LAG <= i < TILES + LAG:
                    gates_t(i - LAG)
                if 1 <= i <= TILES:
                    values(i - 1)
                if LAG <= i < TILES + LAG:
                    logits(i - LAG)
                    gates_back(i - LAG)

            pe.wait_ge(table_ready, 1)

            def block_t(b):
                pe.wait_ge(xin_ld[b % 2], 16 * (b // 2 + 1))
                if b >= 1:
                    pe.wait_ge(xlo_ready, b)
                tr(bank[0][:, 0:BLK], xin[:, b % 2, 0:DA], ident_sb[:, :])
                tr(bank[0][:, BLK:2 * BLK], xin[:, b % 2, DA:2 * DA], ident_sb[:, :]).then_inc(xt_done, 1)

            def layer1(b, expert):
                pe.wait_ge(xlo_ready, b + 1)
                for hf in range(2):
                    if b >= 1:
                        pe.wait_ge(gelu_done, 2 * b - 1 + hf)
                    parts = ((xahi, A_HI), (xalo, A_HI), (xahi, A_LO), (xb1, B_HI), (xb2, B_LO))
                    for i, (x, c) in enumerate(parts):
                        rows = x.shape[0]
                        w = we[0:rows, bass.ds(expert, 1), c + hf * FH:c + hf * FH + FH].rearrange("p e c -> p (e c)")
                        last = mm(bank[1 + hf][:, 0:FH], x[:, :], w, start=(i == 0), stop=(i == 4))
                    last.then_inc(l1_done, 1)

            def hidden_t(b):
                for q, (f0, f1) in enumerate(((0, 4), (4, FC))):
                    pe.wait_ge(gelu_done, 2 * b + 2)
                    if b >= 1:
                        pe.wait_ge(htlo_ready, 2 * b - 1 + q)
                    for f in range(f0, f1):
                        last = tr(bank[3 + q][:, (f - f0) * 128:(f - f0) * 128 + 128], hid[:, f * 128:f * 128 + 128],
                                  ident_sb[:, :])
                    last.then_inc(ht_done, 1)

            def layer2(b, expert):
                if b >= 2:
                    pe.wait_ge(y_ready, b - 1)
                o = bank[6 + b % 2]
                for f in range(FC):
                    if f in (0, 4):
                        pe.wait_ge(htlo_ready, 2 * b + 1 + (f == 4))
                    c = W2_HL + f * 2 * D
                    w = we[:, bass.ds(expert, 1), c:c + 2 * D].rearrange("p e c -> p (e c)")
                    mm(o[:, 0:2 * D], hthi[:, f, :], w, start=(f == 0), stop=False)
                    w = we[:, bass.ds(expert, 1), c:c + D].rearrange("p e c -> p (e c)")
                    last = mm(o[:, 0:D], htlo[:, f, :], w, start=False, stop=(f == FC - 1))
                last.then_inc(l2_done, 1)

            def expert_of(b):
                return pe.value_load(tablei[0:1, T_EXP + b:T_EXP + b + 1], min_val=0, max_val=E - 1)

            pe.wait_ge(early_free, 1)
            block_t(0)
            pe.wait_ge(lo_dve, E - EARLY)
            pe.wait_ge(lo_pool, E + EARLY)
            pe.wait_ge(b1_rows, 64)
            expert = expert_of(0)
            layer1(0, expert)
            block_t(1)
            for b in range(NB):
                hidden_t(b)
                following = expert
                if b + 1 < NB:
                    following = expert_of(b + 1)
                    layer1(b + 1, following)
                if b + 2 < NB:
                    block_t(b + 2)
                layer2(b, expert)
                expert = following

        @block.scalar
        def _(act):
            fn = nc.scalar.activation

            def copy_normal_t(t, da, dbuf, rnd, bk, c0, c1):
                n = ROWS[t]
                act.wait_ge(hnt_done, rnd * TILES + t + 1)
                fn(da, bk[0:DA, c0:c0 + n], ACT.Copy)
                fn(dbuf, bk[0:DB, c1:c1 + n], ACT.Copy).then_inc(hnt_copied, 1)

            for t in range(TILES):
                n = ROWS[t]
                act.wait_ge(embed_done, t + 1)
                fn(h[0:n, t, :], bank[t][0:n, 0:D], ACT.Copy).then_inc(h_copied, 1)

            def first_t(t):
                if t == 0:
                    act.wait_ge(embed_done, TILES)
                if t >= 2:
                    act.wait_ge(v_done, t - 1)
                copy_normal_t(t, hnta[:, t % 2, 0:ROWS[t]], hntb[:, t % 2, 0:ROWS[t]], 0, bank[4 + t % 2],
                              0, 128)

            def v_parts(t):
                n, b = ROWS[t], t % 2
                act.wait_ge(v_done, t + 1)
                fn(vp[0:n, t, :, 0:HD], bank[2 + b][0:n, 0:D].rearrange("p (h d) -> p h d", d=HD), ACT.Copy)\
                    .then_inc(v1_ready, 1)
                act.wait_ge(vr_ready, t + 1)
                fn(vp[0:n, t, :, HD + 1:PC], vr[0:n, b, :].rearrange("p (h d) -> p h d", d=HD), ACT.Copy)\
                    .then_inc(v2_ready, 1)

            first_t(0)
            for t in range(TILES):
                if t + 1 < TILES:
                    first_t(t + 1)
                v_parts(t)

            def copy_q(t):
                n, b = ROWS[t], t % 2
                act.wait_ge(qkt_done, t + 1)
                if t >= 2:
                    act.wait_ge(s_done, GROUPS * (t - 1))
                fn(qta[:, b, 0:n], bank[6][0:DA, 0:n], ACT.Copy)
                fn(qtb[:, b, 0:n], bank[6][0:DB, 2 * TOK:2 * TOK + n], ACT.Copy).then_inc(qt_copied, 1)

            def exps(t, g):
                n, b = ROWS[t], t % 2
                act.wait_ge(max_ready, GROUPS * t + g + 1)
                if t >= 2:
                    act.wait_ge(pt_done, GROUPS * (t - 2) + g + 1)
                for j in range(HG):
                    hd = HG * g + j
                    last = fn(probs[0:n, b, hd, 0:n], bank[g][0:n, TOK * j:TOK * j + n], ACT.Exp,
                              bias=sneg[0:n, b, hd:hd + 1], scale=float(HD) ** -0.5)
                last.then_inc(p_ready, 1)

            def high(t, g):
                n, b = ROWS[t], t % 2
                i = GROUPS * t + g
                act.wait_ge(pt_done, i + 1)
                if t >= 2:
                    act.wait_ge(pv_done, t - 1)
                fn(pth[0:n, b, HG * g:HG * g + HG, 0:n],
                   bank[3 + i % 2][0:n, 0:HG * TOK].rearrange("p (h s) -> p h s", s=TOK)[:, :, 0:n], ACT.Copy)\
                    .then_inc(pth_ready, 1)

            def copy_attended(t):
                n, b = ROWS[t], t % 2
                act.wait_ge(aot_done, t + 1)
                if t >= 2:
                    act.wait_ge(wo_done, t - 1)
                fn(aota[:, b, 0:n], bank[7][0:DA, 0:n], ACT.Copy)
                fn(aotb[:, b, 0:n], bank[7][0:DB, TOK:TOK + n], ACT.Copy).then_inc(aot_copied, 1)

            def copy_second(t):
                n, b = ROWS[t], t % 2
                if t >= 2:
                    act.wait_ge(lg_done, t - 1)
                copy_normal_t(t, hn2ta[:, b, 0:n], hn2tb[0:DB, b, 0:n], 1, bank[5], G0, G1)

            def gate_exp(t):
                n = ROWS[t]
                act.wait_ge(gneg_ready, t + 1)
                fn(gexp[0:n, t, :], gmax[0:n, t, :], ACT.Exp, bias=gneg[0:n, t:t + 1],
                   accum_out=gsum[0:n, t:t + 1]).then_inc(gexp_ready, 1)

            def copy_gates(t):
                n, b = ROWS[t], t % 2
                act.wait_ge(combt_done, t + 1)
                if t >= 2:
                    act.wait_ge(bias_done, t - 1)
                fn(combt[:, b, 0:n], bank[5][0:E, CT:CT + n], ACT.Copy).then_inc(combt_copied, 1)

            def round_weights(e):
                act.wait_ge(w_raw[e], 64)
                hl = we[:, e, W2_HL:WCOLS].rearrange("p (f c) -> p f c", c=2 * D)
                whole = raw[e][:, W2_HL:WCOLS].rearrange("p (f c) -> p f c", c=2 * D)
                fn(we[:, e, A_HI:A_HI + F], raw[e][:, A_LO:A_LO + F], ACT.Copy)
                fn(we[:, e, B_HI:B_HI + F], raw[e][:, B_HI:B_HI + F], ACT.Copy).then_inc(hi_ready, 1)
                fn(hl[:, :, 0:D], whole[:, :, D:2 * D], ACT.Copy).then_inc(hi_ready, 1)

            copy_q(0)
            for i in range(TILES + LAG):
                if 1 <= i <= TILES:
                    high(i - 1, 0)
                if 2 <= i < TILES + 2:
                    copy_attended(i - 2)
                if 1 <= i <= TILES:
                    high(i - 1, 1)
                if i + 1 < TILES:
                    copy_q(i + 1)
                if 1 <= i <= TILES:
                    high(i - 1, 2)
                if i < TILES:
                    exps(i, 0)
                    exps(i, 1)
                if i >= LAG:
                    copy_second(i - LAG)
                if i < TILES:
                    exps(i, 2)
                if i < EARLY:
                    round_weights(i)
                if i >= LAG:
                    gate_exp(i - LAG)
                    copy_gates(i - LAG)
            for e in range(EARLY, E):
                round_weights(e)

            def tokens_high(b):
                act.wait_ge(xt_done, b + 1)
                if b >= 1:
                    act.wait_ge(l1_done, 2 * b)
                fn(xahi[:, :], bank[0][:, 0:BLK], ACT.Copy)
                fn(xb1[:, :], bank[0][:, BLK:2 * BLK], ACT.Copy)
                fn(xb2[0:DB, :], bank[0][0:DB, BLK:2 * BLK], ACT.Copy).then_inc(xhi_ready, 1)

            def gelu(b):
                for hf in range(2):
                    act.wait_ge(l1_done, 2 * b + hf + 1)
                    if b >= 1:
                        act.wait_ge(ht_done, 2 * b)
                    fn(hid[:, hf * FH:hf * FH + FH], bank[1 + hf][:, 0:FH], ACT.Gelu).then_inc(gelu_done, 1)

            def hidden_high(b):
                for q, (f0, f1) in enumerate(((0, 4), (4, FC))):
                    act.wait_ge(ht_done, 2 * b + q + 1)
                    if b >= 1:
                        act.wait_ge(l2_done, b)
                    fn(hthi[:, f0:f1, :], bank[3 + q][:, 0:(f1 - f0) * 128].rearrange("p (f s) -> p f s", s=128),
                       ACT.Copy).then_inc(hthi_ready, 1)

            def output_cross(b):
                act.wait_ge(l2_done, b + 1)
                act.wait_ge(gate_ready, b + 1)
                if b >= 1:
                    act.wait_ge(y_ready, b)
                fn(y1[:, :], bank[6 + b % 2][:, D:2 * D], ACT.Copy, scale=gblk[:, b:b + 1]).then_inc(y1_ready, 1)

            tokens_high(0)
            tokens_high(1)
            gelu(0)
            for b in range(NB):
                hidden_high(b)
                if b + 1 < NB:
                    gelu(b + 1)
                if b + 2 < NB:
                    tokens_high(b + 2)
                output_cross(b)

        @block.vector
        def _(dve):
            v = nc.vector
            steps = [0]

            def step(ins):
                steps[0] += 1
                ins.then_inc(dve_step, 1)
                dve.wait_ge(dve_step, steps[0])

            def norm_stats(t):
                n = ROWS[t]
                step(v.bn_stats(stats[0:n, t, :], h[0:n, t, :]))
                step(v.bn_aggr(mv[0:n, t, :], stats[0:n, t, :]))
                v.tensor_scalar(veps[0:n, t:t + 1], mv[0:n, t, 1:2], EPS, None, ALU.add).then_inc(veps_ready, 1)

            def norm_apply(t, rnd):
                n = ROWS[t]
                c = slice(t, t + 1)
                dve.wait_ge(rstd_ready, rnd * TILES + t + 1)
                if rnd == 0:
                    v.tensor_scalar(hn[0:n, t, :], h[0:n, t, :], mv[0:n, t, 0:1], rstd[0:n, c], ALU.subtract,
                                    ALU.mult).then_inc(hn_ready, 1)
                    return
                if t >= 3:
                    dve.wait_ge(scattered[t % 3], 32 * (t // 3))
                v.tensor_scalar(pay[0:n, t % 3, 0:D], h[0:n, t, :], mv[0:n, t, 0:1], rstd[0:n, c], ALU.subtract,
                                ALU.mult)
                v.tensor_copy(pay[0:n, t % 3, C_TOK:C_TOK + 1].bitcast(U32), tokids_sb[0:n, t:t + 1])
                v.tensor_scalar(pay[0:n, t % 3, D:D + DB], h[0:n, t, DA:D], mv[0:n, t, 0:1], rstd[0:n, c],
                                ALU.subtract, ALU.mult).then_inc(hn_ready, 1)

            v.memset(nhalf[:, :], -0.5).then_inc(fixed, 1)
            v.memset(hn2tb[DB:DB + 1, :, :], 1.0).then_inc(fixed, 1)

            def split_w1(e):
                dve.wait_ge(hi_ready, 2 * e + 1)
                v.tensor_tensor(we[:, e, A_LO:A_LO + F], raw[e][:, A_LO:A_LO + F], we[:, e, A_HI:A_HI + F],
                                ALU.subtract)
                v.tensor_tensor(we[0:DB, e, B_LO:B_LO + F], raw[e][0:DB, B_LO:B_LO + F],
                                we[0:DB, e, B_HI:B_HI + F], ALU.subtract).then_inc(lo_dve, 1)

            for t in range(TILES + 1):
                if t < TILES:
                    dve.wait_ge(h_copied, t + 1)
                    norm_stats(t)
                if t >= 1:
                    norm_apply(t - 1, 0)

            dve.wait_ge(b1_raw, 16)
            step(v.tensor_copy(b1hi_sb[:, :], b1raw_sb[:, :]))
            v.tensor_tensor(b1lo_sb[:, :], b1raw_sb[:, :], b1hi_sb[:, :], ALU.subtract).then_inc(b1_lo, 1)

            dve.wait_ge(ld_attn, ATTN_LOADS)
            for t in range(TILES):
                n, b = ROWS[t], t % 2
                dve.wait_ge(qk_done, t + 1)
                if t >= 2:
                    dve.wait_ge(qk_ready, t - 1)
                x = bank[6 + b][0:n, 0:2 * D].rearrange("p (a c) -> p a c", a=2)
                v.tensor_tensor(ropec[0:n, b, :].rearrange("p (a c) -> p a c", a=2), x,
                                cos_sb[0:n, :].unsqueeze(1).to_broadcast([n, 2, D]), ALU.mult)
                x = bank[6 + b][0:n, 0:2 * D].rearrange("p (c s) -> p c s", s=2)
                turned = ropes[0:n, b, :].rearrange("p (c s) -> p c s", s=2)
                sn = sin_sb[0:n, :].rearrange("p (c s) -> p c s", s=2)
                for a in range(2):
                    for s in range(2):
                        cs = slice(a * D // 2, (a + 1) * D // 2)
                        last = v.tensor_tensor(turned[:, cs, s], x[:, cs, 1 - s], sn[:, :, s], ALU.mult)
                last.then_inc(rope_ready, 1)
                dve.wait_ge(v_done, t + 1)
                dve.wait_ge(v1_ready, t + 1)
                if t >= 2:
                    dve.wait_ge(v3_ready, t - 1)
                v.tensor_tensor(vr[0:n, b, :].rearrange("p (h d) -> p h d", d=HD),
                                bank[2 + b][0:n, 0:D].rearrange("p (h d) -> p h d", d=HD),
                                vp[0:n, t, :, 0:HD], ALU.subtract).then_inc(vr_ready, 1)

            def spread_k(t):
                n, b = ROWS[t], t % 2
                if t == 0:
                    dve.wait_ge(qk_ready, TILES)
                    dve.wait_ge(v2_ready, TILES)
                    dve.wait_ge(v3_ready, TILES)
                    dve.wait_ge(v_done, TILES)
                dve.wait_ge(qkt_done, t + 1)
                dve.wait_ge(qt_copied, t + 1)
                if t >= 2:
                    dve.wait_ge(s_done, GROUPS * (t - 1))
                v.tensor_tensor(kbda[:, b, :, 0:n], bank[6][0:DA, TOK:TOK + n].unsqueeze(1).to_broadcast([DA, 8, n]),
                                headmask_sb[0:DA, :].unsqueeze(2).to_broadcast([DA, 8, n]), ALU.mult)
                v.tensor_tensor(kbdb[:, b, :, 0:n],
                                bank[6][0:DB, 3 * TOK:3 * TOK + n].unsqueeze(1).to_broadcast([DB, 4, n]),
                                headmask_sb[0:DB, 0:4].unsqueeze(2).to_broadcast([DB, 4, n]), ALU.mult)\
                    .then_inc(kbd_ready, 1)

            def scores_max(t, groups):
                n, b = ROWS[t], t % 2
                for g in groups:
                    hs = slice(HG * g, HG * g + HG)
                    dve.wait_ge(s_done, GROUPS * t + g + 1)
                    if t >= 2:
                        dve.wait_ge(p_ready, GROUPS * (t - 2) + g + 1)
                    s = bank[g][0:n, 0:HG * TOK].rearrange("p (h s) -> p h s", s=TOK)[:, :, 0:n]
                    step(v.tensor_reduce(smax[0:n, b, hs], s, AX.X, ALU.max))
                    v.tensor_scalar(sneg[0:n, b, hs], smax[0:n, b, hs], -float(HD) ** -0.5, None, ALU.mult)\
                        .then_inc(max_ready, 1)

            def low(t, groups):
                n, b = ROWS[t], t % 2
                for g in groups:
                    i = GROUPS * t + g
                    hs = slice(HG * g, HG * g + HG)
                    dve.wait_ge(pth_ready, i + 1)
                    if t >= 2:
                        dve.wait_ge(pv_done, t - 1)
                    v.tensor_tensor(ptl[0:n, b, hs, 0:n],
                                    bank[3 + i % 2][0:n, 0:HG * TOK].rearrange("p (h s) -> p h s", s=TOK)[:, :, 0:n],
                                    pth[0:n, b, hs, 0:n], ALU.subtract).then_inc(ptl_ready, 1)

            def norm_out(t):
                n, b = ROWS[t], t % 2
                dve.wait_ge(pv_done, t + 1)
                if t >= 2:
                    dve.wait_ge(aot_done, t - 1)
                o = bank[7][0:n, 0:HEADS * PC].rearrange("p (h d) -> p h d", d=PC)
                a = ao[0:n, b, :].rearrange("p (h d) -> p h d", d=HD)
                v.reciprocal(rsum[0:n, b, :], o[:, :, HD])
                step(v.tensor_copy(a, o[:, :, 0:HD]))
                step(v.tensor_tensor(a, o[:, :, HD + 1:PC], a, ALU.add))
                v.tensor_tensor(a, a,
                                rsum[0:n, b, :].unsqueeze(2).to_broadcast([n, HEADS, HD]), ALU.mult)\
                    .then_inc(ao_ready, 1)

            def residual(t):
                n = ROWS[t]
                dve.wait_ge(wo_done, t + 1)
                v.tensor_tensor(h[0:n, t, :], bank[7][0:n, 2 * TOK:2 * TOK + D], h[0:n, t, :], ALU.add).then_inc(h2_ready, 1)

            def choose(t):
                n, b = ROWS[t], t % 2
                lg = bank[5][0:n, LG:LG + E]
                dve.wait_ge(lg_done, t + 1)
                step(v.max(gmax[0:n, t, :], lg))
                v.tensor_scalar(gneg[0:n, t:t + 1], gmax[0:n, t, 0:1], -1.0, None, ALU.mult).then_inc(gneg_ready, 1)
                step(v.max_index(gidx[0:n, t, :], gmax[0:n, t, :], lg))
                step(v.tensor_copy(pay[0:n, t % 3, C_IDX:C_IDX + 2], gidx[0:n, t, 0:2]))
                for j in range(2):
                    last = v.tensor_scalar(chosen[0:n, t, j, :], iota_sb[0:n, :], pay[0:n, t % 3, C_IDX + j:C_IDX + j + 1],
                                           None, ALU.is_equal)
                step(last)
                v.tensor_tensor(member[0:n, t, :], chosen[0:n, t, 0, :], chosen[0:n, t, 1, :], ALU.add)\
                    .then_inc(chosen_ready, 1)
                dve.wait_ge(gexp_ready, t + 1)
                step(v.reciprocal(grec[0:n, t:t + 1], gsum[0:n, t:t + 1]))
                step(v.tensor_scalar(pay[0:n, t % 3, C_GATE:C_GATE + 2], gexp[0:n, t, 0:2], grec[0:n, t:t + 1], None,
                                     ALU.mult))
                for j in range(2):
                    last = v.tensor_scalar(comb2[0:n, b, j, :], chosen[0:n, t, j, :],
                                           pay[0:n, t % 3, C_GATE + j:C_GATE + j + 1], None, ALU.mult)
                step(last)
                v.tensor_tensor(comb[0:n, t, :], comb2[0:n, b, 0, :], comb2[0:n, b, 1, :], ALU.add)\
                    .then_inc(comb_ready, 1)

            def rows(t):
                n, b = ROWS[t], t % 2
                dve.wait_ge(rank_done, t + 1)
                step(v.tensor_tensor(rowof[0:n, t, :], bank[5][0:n, LG:LG + E], rowbase_sb[0:n, :], ALU.add))
                step(v.tensor_tensor(rowsel[0:n, b, :, :], chosen[0:n, t, :, :],
                                     rowof[0:n, t, :].unsqueeze(1).to_broadcast([n, 2, E]), ALU.mult))
                step(v.tensor_reduce(rowf[0:n, t, :], rowsel[0:n, b, :, :], AX.X, ALU.add))
                v.tensor_copy(rowu[0:n, t, :], rowf[0:n, t, :]).then_inc(row_ready, 1)

            def add_bias2(t):
                n = ROWS[t]
                dve.wait_ge(bias_done, t + 1)
                v.tensor_tensor(h[0:n, t, :], bank[5][0:n, 0:D], h[0:n, t, :], ALU.add).then_inc(h3_ready, 1)

            spread_k(0)
            for i in range(TILES + LAG + 1):
                if 1 <= i <= TILES:
                    low(i - 1, (0, 1))
                if LAG <= i < TILES + LAG:
                    norm_stats(i - LAG)
                if i + 1 < TILES:
                    spread_k(i + 1)
                if 1 <= i <= TILES:
                    low(i - 1, (2,))
                if i >= LAG + 1:
                    rows(i - LAG - 1)
                if LAG <= i < TILES + LAG:
                    norm_apply(i - LAG, 1)
                if i < TILES:
                    scores_max(i, (0, 1))
                if LAG + 1 <= i < TILES + LAG:
                    add_bias2(i - LAG - 1)
                if 2 <= i < TILES + 2:
                    residual(i - 2)
                if i < TILES:
                    scores_max(i, (2,))
                if 1 <= i <= TILES:
                    norm_out(i - 1)
                if i == TILES:
                    v.memset(xb2[DB:DB + 2, :].bitcast(F32), 1.0).then_inc(early_free, 1)
                if LAG <= i < TILES + LAG:
                    choose(i - LAG)

            dve.wait_ge(count_done, 1)
            step(v.tensor_tensor(over[:, :, :], bank[0][:, 0:E].unsqueeze(2).to_broadcast([128, E, MAXB]),
                                 steps_sb[:, :].unsqueeze(1).to_broadcast([128, E, MAXB]), ALU.is_gt))
            step(v.tensor_reduce(blocks[:, :], over[:, :, :], AX.X, ALU.add))
            v.tensor_scalar(rest[:, :], blocks[:, :], -float(BLK), float(CAP), ALU.mult, ALU.add)
            step(v.tensor_tensor(blocks8[:, :, :], lower8_sb[:, :, :],
                                 blocks[:, :].unsqueeze(1).to_broadcast([128, E, E]), ALU.mult))
            step(v.tensor_reduce(ends[:, :], blocks8[:, :, :], AX.X, ALU.add))
            step(v.tensor_tensor(passed[:, 0, :, :], blockids_sb[:, :].unsqueeze(2).to_broadcast([128, NB, E]),
                                 ends[:, :].unsqueeze(1).to_broadcast([128, NB, E]), ALU.is_ge))
            step(v.tensor_tensor(passed[:, 1, :, :], passed[:, 0, :, :],
                                 rest[:, :].unsqueeze(1).to_broadcast([128, NB, E]), ALU.mult))
            step(v.tensor_reduce(tmp_nb[:, :, :], passed[:, :, :, :], AX.X, ALU.add))
            step(v.scalar_tensor_tensor(out=tmp_nb[:, 1, :], in0=blockids_sb[:, :], scalar=float(BLK),
                                        in1=tmp_nb[:, 1, :], op0=ALU.mult, op1=ALU.add))
            v.tensor_scalar(table[:, :], tmp_nb[:, 0, :], float(E - 1), None, ALU.min)
            v.tensor_scalar(tablei[:, T_EXP:T_EXP + NB], tmp_nb[:, 0, :], float(E - 1), None, ALU.min)
            v.tensor_scalar(tablei[:, T_ROW:T_ROW + NB], tmp_nb[:, 1, :], float(SPARE), None, ALU.min)\
                .then_inc(table_ready, 1)

            add_bias2(TILES - 1)

            for e in range(EARLY, E):
                split_w1(e)

            def tokens_low(b):
                dve.wait_ge(xhi_ready, b + 1)
                v.tensor_tensor(xalo[:, :], bank[0][:, 0:BLK], xahi[:, :], ALU.subtract)
                v.tensor_tensor(xb1[DB:128, :], bank[0][DB:128, BLK:2 * BLK], xb1[DB:128, :], ALU.subtract)\
                    .then_inc(xlo_ready, 1)

            def block_gates(b):
                x = xin[:, b % 2, :]
                dve.wait_ge(xin_ld[b % 2], 16 * (b // 2 + 1))
                v.tensor_copy(tokblk[:, b:b + 1], x[:, C_TOK:C_TOK + 1].bitcast(U32))
                step(v.scalar_tensor_tensor(out=gsel[:, b % 2, :], in0=x[:, C_IDX:C_IDX + 2],
                                            scalar=table[:, b:b + 1], in1=x[:, C_GATE:C_GATE + 2],
                                            op0=ALU.is_equal, op1=ALU.mult))
                v.tensor_tensor(gblk[:, b:b + 1], gsel[:, b % 2, 0:1], gsel[:, b % 2, 1:2], ALU.add).then_inc(gate_ready, 1)

            def hidden_low(b):
                for q, (f0, f1) in enumerate(((0, 4), (4, FC))):
                    dve.wait_ge(hthi_ready, 2 * b + q + 1)
                    v.tensor_tensor(htlo[:, f0:f1, :],
                                    bank[3 + q][:, 0:(f1 - f0) * 128].rearrange("p (f s) -> p f s", s=128),
                                    hthi[:, f0:f1, :], ALU.subtract).then_inc(htlo_ready, 1)

            def output(b):
                dve.wait_ge(y1_ready, b + 1)
                if b >= 2:
                    dve.wait_ge(added, 16 * (b - 1))
                v.scalar_tensor_tensor(out=y[:, b % 2, :], in0=bank[6 + b % 2][:, 0:D], scalar=gblk[:, b:b + 1],
                                       in1=y1[:, :], op0=ALU.mult, op1=ALU.add).then_inc(y_ready, 1)

            block_gates(0)
            tokens_low(0)
            block_gates(1)
            tokens_low(1)
            for b in range(NB):
                hidden_low(b)
                if b + 2 < NB:
                    block_gates(b + 2)
                    tokens_low(b + 2)
                output(b)


def constants():
    import numpy as np
    bf16 = mybir.dt.np(BF16)
    i = np.arange(D // 2, dtype=np.float64)
    theta = 10000.0 ** (-2.0 * i / D)
    m_theta = np.repeat(np.arange(1, SEQ + 1, dtype=np.float64)[:, None] * theta[None, :], 2, axis=-1)
    pos = np.arange(TOK) % SEQ
    sign = np.where(np.arange(D) % 2 == 0, -1.0, 1.0)
    img = np.arange(TOK) // SEQ
    allowed = (img[:, None] == img[None, :]) & (pos[None, :] <= pos[:, None])
    tok = np.arange(N)
    pad = np.zeros((BLK, PAY), np.float32)
    pad[:, C_TOK] = np.arange(N, N + BLK, dtype=np.uint32).view(np.float32)
    return {
        "tok_sel": np.stack([tok % SEQ != 0, tok % SEQ == 0]).astype(np.float32),
        "rope_cos": np.cos(m_theta).astype(np.float32)[pos],
        "rope_sin": (np.sin(m_theta).astype(np.float32)[pos] * sign).astype(np.float32),
        "mask": np.where(allowed, 0.0, -1e30).astype(bf16),
        "ident": np.eye(128, dtype=np.float32),
        "ident_half": np.eye(128, dtype=np.float32).astype(bf16),
        "head_mask": (np.arange(128)[:, None] // HD == np.arange(8)[None, :]).astype(np.float32),
        "iota8": np.tile(np.arange(E, dtype=np.float32), (128, 1)),
        "before": (np.arange(TOK)[:, None] < np.arange(TOK)[None, :]).astype(np.float32).astype(bf16),
        "ones_half": np.ones((TOK, 128), np.float32).astype(bf16),
        "tok_ids": (np.arange(TILES)[None, :] * TOK + np.arange(TOK)[:, None]).astype(np.uint32),
        "pad_rows": pad,
        "row_base": np.tile(CAP * np.arange(E, dtype=np.float32), (128, 1)),
        "block_steps": np.tile(BLK * np.arange(MAXB, dtype=np.float32), (128, 1)),
        "lower8": np.tile(np.tril(np.ones((E, E), np.float32))[None], (128, 1, 1)),
        "block_ids": np.tile(np.arange(NB, dtype=np.float32), (128, 1)),
    }


def laid_out(x, cls_tok, L0_tok_W, L0_tok_b, L0_attn_W_q, L0_attn_W_k, L0_attn_W_v, L0_attn_W_o, L0_ffn_Wg,
             L0_ffn_bg, L0_ffn_W1, L0_ffn_b1, L0_ffn_W2, L0_ffn_b2):
    import numpy as np
    a = [np.asarray(v) for v in (x, cls_tok, L0_tok_W, L0_tok_b, L0_attn_W_q, L0_attn_W_k, L0_attn_W_v, L0_attn_W_o,
                                 L0_ffn_Wg, L0_ffn_bg, L0_ffn_W1, L0_ffn_b1, L0_ffn_W2, L0_ffn_b2)]
    x, cls_tok, wt, bt, wq, wk, wv, wo, wg, bg, w1, b1, w2, b2 = a
    p = 16
    g = x.shape[2] // p
    cols = np.zeros((TILES * TOK, KC * 128), x.dtype).reshape(TILES * TOK, -1)
    body = x.reshape(IMAGES, 3, g, p, g, p).transpose(0, 2, 4, 1, 3, 5).reshape(IMAGES, g * g, -1)
    cols[:N].reshape(IMAGES, SEQ, -1)[:, 1:] = body
    wqkv = np.concatenate([wq.T, wk.T, wv.T], axis=1)
    return {
        "patches": cols.reshape(TILES, TOK, KC, 128).transpose(0, 3, 2, 1),
        "w_tok": wt.reshape(D, KC, 128).transpose(2, 1, 0),
        "tok_rows": np.stack([bt, cls_tok.reshape(D)]),
        "w_qkv_a": wqkv[:DA], "w_qkv_b": wqkv[DA:],
        "w_o_a": wo.T[:DA], "w_o_b": wo.T[DA:],
        "w_g_a": wg[:DA], "w_g_b": np.concatenate([wg[DA:], bg[None]]),
        "w1_a": w1[:, :DA].transpose(1, 0, 2), "w1_b": w1[:, DA:].transpose(1, 0, 2),
        "w1_bb": np.concatenate([w1[:, DA:], w1[:, DA:]], axis=1).transpose(1, 0, 2),
        "b1": b1,
        "w2": w2.reshape(E, FC, 128, D).transpose(2, 0, 1, 3),
        "b2": b2,
    }


_INS = ["patches", "w_tok", "tok_rows", "tok_sel", "w_qkv_a", "w_qkv_b", "rope_cos", "rope_sin", "mask", "ident",
        "ident_half", "head_mask", "w_o_a", "w_o_b", "w_g_a", "w_g_b", "iota8", "w1_a", "w1_bb", "w1_b", "b1", "w2",
        "b2", "before", "ones_half", "tok_ids", "pad_rows", "row_base", "block_steps", "lower8", "block_ids"]


def kernel(**inputs):
    import numpy as np
    import concourse.bacc as bacc
    from concourse.bass_utils import run_bass_kernel_spmd

    nc = bacc.Bacc("TRN2", target_bir_lowering=False, num_devices=1)
    given = {**constants(), **laid_out(**inputs)}
    arrays, args = {}, []
    for name in _INS:
        a = np.ascontiguousarray(given[name])
        arrays[f"in_{name}"] = a
        args.append(nc.dram_tensor(f"in_{name}", a.shape, mybir.dt.from_np(a.dtype), kind="ExternalInput").ap())
    out = nc.dram_tensor("out_y", (N + BLK, D), F32, kind="ExternalOutput").ap()
    vit_block(nc, *args, out)
    r = run_bass_kernel_spmd(nc, [arrays], core_ids=[0])
    return r.results[0]["out_y"][:N].reshape(IMAGES, SEQ, D)
```

```python
import concourse.bass as bass
from concourse import mybir
from contextlib import ExitStack, nullcontext

F32 = mybir.dt.float32
BF16 = mybir.dt.bfloat16
FP16 = mybir.dt.float16
F32R = mybir.dt.float32r
I32 = mybir.dt.int32
U32 = mybir.dt.uint32
ALU = mybir.AluOpType
ACT = mybir.ActivationFunctionType
AX = mybir.AxisListType

IMAGES = 16
SEQ = 37
GROUP = 3
TOK = GROUP * SEQ
N = IMAGES * SEQ
TILES = -(-N // TOK)
ROWS = [min(TOK, N - t * TOK) for t in range(TILES)]
D = 192
DA, DB = 128, D - 128
HEADS, HD = 12, 16
HG = 4
GROUPS = HEADS // HG
KC = 6
E = 8
F = 768
FC = F // 128
EPS = 1e-5

BLK = 128
CAP = -(-N // BLK) * BLK
MAXB = CAP // BLK
SPARE = E * CAP
NB = (2 * N - E) // BLK + E
MINB = -(-2 * N // BLK)
C_TOK, C_IDX, C_GATE, PAY = 256, 257, 259, 261
A_HI, A_LO, B_HI, B_LO, W2_HL = 0, F, 2 * F, 3 * F, 4 * F
WCOLS = 4 * F + FC * 2 * D
EARLY = 6
VC = 3 * HD + 1
G0, G1, LG, CT = 0, TOK, 2 * TOK, 256
PC = 2 * HD + 1
BLOCK_WARM_UP = 18
WPARTS = 3
FH = F // 2
LAG = 3
T_EXP, T_ROW, T_LIVE, T_COLS = 0, NB, 2 * NB, 2 * NB + 1


class Region:

    def __init__(self, nc, at, end):
        self.nc, self.at, self.end = nc, at, end

    def __call__(self, name, shape, dt=F32):
        size = mybir.dt.size(dt)
        for n in shape[1:]:
            size *= n
        t = self.nc.alloc_sbuf_tensor_at(name, shape, dt, offset=self.at)
        self.at += -(-size // 32) * 32
        assert self.at <= self.end, (name, self.at, self.end)
        return t


def vit_block(nc, patches, w_tok, tok_rows, tok_sel, w_qkv_a, w_qkv_b, rope_cos, rope_sin, mask,
              ident, ident_half, head_mask, w_o_a, w_o_b, w_g_a, w_g_b, iota8, w1_a, w1_bb, w1_b, b1, w2, b2,
              before, ones_half, tok_ids, pad_rows, row_base, block_steps, lower8, block_ids, out):
    xs = nc.dram_tensor("dispatched", (SPARE + BLK, PAY), F32, kind="Internal").ap()
    ctx = ExitStack()
    with ctx:
        def sem(name):
            return ctx.enter_context(nc.semaphore(name))

        bank = [ctx.enter_context(nc.psum_tensor(f"bank{i}", [128, 512], F32)) for i in range(8)]
        slab = ctx.enter_context(nc.sbuf_tensor("slab", [128, (nc.sbuf_bytes_remaining - 64) // 4], F32))
        start = -(-(nc.sbuf_base - slab.shape[1] * 4) // 32) * 32
        top = nc.sbuf_base

        gates_bank = [bank[5]] * (TILES - 2) + [bank[1], bank[2]]

        keep = Region(nc, start, top)
        ident_sb = keep("ident_sb", [128, 128])
        identh_sb = keep("identh_sb", [128, 128], BF16)
        headmask_sb = keep("headmask_sb", [128, 8])
        woa_sb = keep("woa_sb", [DA, D])
        wob_sb = keep("wob_sb", [DB, D])
        wga_sb = keep("wga_sb", [DA, E])
        wgb_sb = keep("wgb_sb", [DB + 1, E])
        iota_sb = keep("iota_sb", [128, E])
        b2_sb = keep("b2_sb", [E, D])
        before_sb = keep("before_sb", [TOK, TOK], BF16)
        onesh_sb = keep("onesh_sb", [TOK, 128], BF16)
        tokids_sb = keep("tokids_sb", [TOK, TILES], U32)
        rowbase_sb = keep("rowbase_sb", [128, E])
        steps_sb = keep("steps_sb", [128, MAXB])
        lower8_sb = keep("lower8_sb", [128, E, E])
        blockids_sb = keep("blockids_sb", [128, NB])
        b1lo_sb = keep("b1lo_sb", [E, F], F32R)
        h = keep("h", [TOK, TILES, D])
        stats = keep("stats", [TOK, TILES, 6])
        mv = keep("mv", [TOK, TILES, 2])
        veps = keep("veps", [TOK, TILES])
        rstd = keep("rstd", [TOK, TILES])
        nhalf = keep("nhalf", [128, 1])
        preload = keep("preload", [128, 1])
        ao = keep("ao", [TOK, 2, D])
        aota = keep("aota", [DA, 2, TOK])
        aotb = keep("aotb", [DB, 2, TOK])
        smax = keep("smax", [TOK, 2, HEADS])
        sneg = keep("sneg", [TOK, 2, HEADS])
        rsum = keep("rsum", [TOK, 2, HEADS])
        hn2ta = keep("hn2ta", [DA, 2, TOK])
        hn2tb = keep("hn2tb", [DB + 1, 2, TOK])
        combt = keep("combt", [E, 3, TOK])
        pay = keep("pay", [TOK, 3, PAY])
        gmax = keep("gmax", [TOK, TILES, 8])
        gidx = keep("gidx", [TOK, TILES, 8], U32)
        gneg = keep("gneg", [TOK, TILES])
        gexp = keep("gexp", [TOK, TILES, 8])
        gsum = keep("gsum", [TOK, TILES])
        grec = keep("grec", [TOK, TILES])
        chosen = keep("chosen", [TOK, TILES, 2, E])
        member = keep("member", [TOK, TILES, E], BF16)
        comb2 = keep("comb2", [TOK, 2, 2, E])
        comb = keep("comb", [TOK, TILES, E])
        rowof = keep("rowof", [TOK, TILES, E])
        rowsel = keep("rowsel", [TOK, 2, 2, E])
        rowf = keep("rowf", [TOK, TILES, 2])
        rowu = keep("rowu", [TOK, TILES, 2], U32)
        blocks = keep("blocks", [128, E])
        ends = keep("ends", [128, E])
        table = keep("table", [128, NB])
        tablei = keep("tablei", [128, T_COLS], I32)

        w_at = keep.at
        we = Region(nc, w_at, top)("we", [128, E, WCOLS], F32R)
        raw = [Region(nc, w_at + e * WCOLS * 4, top)(f"raw{e}", [128, WCOLS], F32) for e in range(E)]
        moe = Region(nc, w_at + E * WCOLS * 4, top)
        xin = moe("xin", [BLK, 2, PAY])
        xahi = moe("xahi", [DA, BLK], F32R)
        xalo = moe("xalo", [DA, BLK], F32R)
        xb1 = moe("xb1", [128, BLK], F32R)
        xb2 = moe("xb2", [DB + 2, BLK], F32R)
        scratch = Region(nc, moe.at, top)
        over = scratch("over", [128, E, MAXB])
        blocks8 = scratch("blocks8", [128, E, E])
        passed = scratch("passed", [128, 2, NB, E])
        rest = scratch("rest", [128, E])
        tmp_nb = scratch("tmp_nb", [128, 2, NB])
        hid = moe("hid", [BLK, F])
        hthi = moe("hthi", [128, FC, BLK], F32R)
        htlo = moe("htlo", [128, FC, BLK], F32R)
        y1 = moe("y1", [BLK, D])
        y = moe("y", [BLK, 2, D])
        gsel = moe("gsel", [BLK, 2, 2])
        gblk = moe("gblk", [BLK, NB])
        tokblk = moe("tokblk", [BLK, NB], U32)

        early = Region(nc, w_at + EARLY * WCOLS * 4, top)
        wqkva_sb = early("wqkva_sb", [DA, 3 * D])
        wqkvb_sb = early("wqkvb_sb", [DB, 3 * D])
        cos_sb = early("cos_sb", [TOK, D])
        sin_sb = early("sin_sb", [TOK, D])
        mask_sb = early("mask_sb", [TOK, TOK], BF16)
        qk = early("qk", [TOK, TILES, 2 * D])
        vp = early("vp", [TOK, TILES, HEADS, VC], BF16)
        qta = early("qta", [DA, 2, TOK])
        qtb = early("qtb", [DB, 2, TOK])
        first = Region(nc, early.at, top)
        x_sb = first("x_sb", [128, TILES, KC, TOK])
        wtok_sb = first("wtok_sb", [128, KC, D])
        tokrows_sb = first("tokrows_sb", [2, D])
        toksel_sb = first("toksel_sb", [2, N])
        b1raw_sb = first("b1raw_sb", [E, F])
        b1hi_sb = first("b1hi_sb", [E, F], F32R)
        second = Region(nc, early.at, top)
        probs = second("probs", [TOK, 2, HEADS, TOK])
        pth = second("pth", [TOK, 2, HEADS, TOK], FP16)
        ptl = second("ptl", [TOK, 2, HEADS, TOK], FP16)
        third = Region(nc, first.at, top)
        hn = third("hn", [TOK, TILES, D])
        project = Region(nc, early.at, first.at)
        hnta = project("hnta", [DA, 2, TOK])
        hntb = project("hntb", [DB, 2, TOK])
        ropec = project("ropec", [TOK, 2, 2 * D])
        ropes = project("ropes", [TOK, 2, 2 * D])
        vr = project("vr", [TOK, 2, D])
        fourth = Region(nc, second.at, third.at)
        kbda = fourth("kbda", [DA, 2, 8, TOK])
        kbdb = fourth("kbdb", [DB, 2, 4, TOK])

        ld_x = [sem(f"ld_x{t}") for t in range(TILES)]
        ld_w = [sem(f"ld_w{c}") for c in range(WPARTS)]
        ld_embed = sem("ld_embed")
        ld_attn = sem("ld_attn")
        ld_const = sem("ld_const")
        ld_rest = sem("ld_rest")
        embed_done = sem("embed_done")
        h_copied = sem("h_copied")
        veps_ready = sem("veps_ready")
        rstd_ready = sem("rstd_ready")
        hn_ready = sem("hn_ready")
        hnt_done = sem("hnt_done")
        hnt_copied = sem("hnt_copied")
        qk_done = sem("qk_done")
        v_done = sem("v_done")
        rope_ready = sem("rope_ready")
        qk_ready = sem("qk_ready")
        v1_ready = sem("v1_ready")
        vr_ready = sem("vr_ready")
        v2_ready = sem("v2_ready")
        v3_ready = sem("v3_ready")
        ones_ready = sem("ones_ready")
        qkt_done = sem("qkt_done")
        qt_copied = sem("qt_copied")
        kbd_ready = sem("kbd_ready")
        s_done = sem("s_done")
        max_ready = sem("max_ready")
        p_ready = sem("p_ready")
        pt_done = sem("pt_done")
        pth_ready = sem("pth_ready")
        ptl_ready = sem("ptl_ready")
        pv_done = sem("pv_done")
        ao_ready = sem("ao_ready")
        aot_done = sem("aot_done")
        aot_copied = sem("aot_copied")
        wo_done = sem("wo_done")
        h2_ready = sem("h2_ready")
        h3_ready = sem("h3_ready")
        lg_done = sem("lg_done")
        gneg_ready = sem("gneg_ready")
        gexp_ready = sem("gexp_ready")
        comb_ready = sem("comb_ready")
        combt_done = sem("combt_done")
        combt_copied = sem("combt_copied")
        bias_done = sem("bias_done")
        chosen_ready = sem("chosen_ready")
        rank_done = sem("rank_done")
        row_ready = sem("row_ready")
        scattered = [sem(f"scattered{b}") for b in range(3)]
        out_first = sem("out_first")
        count_done = sem("count_done")
        table_ready = sem("table_ready")
        padded = sem("padded")
        w1_hi = sem("w1_hi")
        w2_hi = sem("w2_hi")
        w_raw = [sem(f"w_raw{e}") for e in range(E)]
        b1_raw = sem("b1_raw")
        b1_lo = sem("b1_lo")
        b1_rows = sem("b1_rows")
        lo_dve = sem("lo_dve")
        lo_pool = sem("lo_pool")
        early_free = sem("early_free")
        xin_ld = [sem(f"xin_ld{b}") for b in range(2)]
        xt_done = sem("xt_done")
        xhi_ready = sem("xhi_ready")
        xlo_ready = sem("xlo_ready")
        gate_ready = sem("gate_ready")
        l1_done = sem("l1_done")
        gelu_done = sem("gelu_done")
        ht_done = sem("ht_done")
        hthi_ready = sem("hthi_ready")
        htlo_ready = sem("htlo_ready")
        l2_done = sem("l2_done")
        y1_ready = sem("y1_ready")
        y_ready = sem("y_ready")
        added = sem("added")
        fixed = sem("fixed")
        dve_step = sem("dve_step")

        ATTN_LOADS = 16 * 4
        REST_LOADS = 16 * 15

        def blocks_in_use(engine):
            engine.wait_ge(table_ready, 1)
            live = engine.value_load(tablei[0:1, T_LIVE:T_LIVE + 1], min_val=MINB, max_val=NB)
            return lambda b: engine.If(live > b) if b >= MINB else nullcontext()

        block = ctx.enter_context(nc.Block())

        @block.sync
        def _(sp):
            for c in range(WPARTS):
                ks = slice(c * KC // WPARTS, (c + 1) * KC // WPARTS)
                sp.dma_start(x_sb[:, 0, ks, :], patches[0][:, ks, :]).then_inc(ld_w[c], 16)
                sp.dma_start(wtok_sb[:, ks, :], w_tok[:, ks, :]).then_inc(ld_w[c], 16)
            sp.dma_start(tokrows_sb[:, :], tok_rows).then_inc(ld_embed, 16)
            sp.dma_start(toksel_sb[:, :], tok_sel).then_inc(ld_embed, 16)
            for t in range(1, TILES):
                sp.dma_start(x_sb[:, t], patches[t]).then_inc(ld_x[t], 16)
            sp.dma_start(ident_sb[:, :], ident).then_inc(ld_const, 16)
            sp.dma_start(identh_sb[:, :], ident_half).then_inc(ld_const, 16)
            for dst, src in ((wqkva_sb, w_qkv_a), (wqkvb_sb, w_qkv_b), (cos_sb, rope_cos), (sin_sb, rope_sin)):
                sp.dma_start(dst[:, :], src).then_inc(ld_attn, 16)
            for dst, src in ((mask_sb, mask), (headmask_sb, head_mask), (woa_sb, w_o_a), (wob_sb, w_o_b),
                             (wga_sb, w_g_a), (wgb_sb, w_g_b), (iota_sb, iota8), (before_sb, before),
                             (onesh_sb, ones_half), (tokids_sb, tok_ids), (rowbase_sb, row_base),
                             (steps_sb, block_steps), (lower8_sb, lower8), (blockids_sb, block_ids), (b2_sb, b2)):
                sp.dma_start(dst[:], src).then_inc(ld_rest, 16)
            sp.dma_start(b1raw_sb[:, :], b1).then_inc(b1_raw, 16)

            def load_raw(e):
                sp.dma_start(raw[e][:, A_LO:A_LO + F], w1_a[:, e, :]).then_inc(w_raw[e], 16)
                sp.dma_start(raw[e][0:DB, B_LO:B_LO + F], w1_b[:, e, :]).then_inc(w_raw[e], 16)
                sp.dma_start(raw[e][:, B_HI:B_HI + F], w1_bb[:, e, :]).then_inc(w_raw[e], 16)
                sp.dma_start(raw[e][:, W2_HL:WCOLS].rearrange("p (f c) -> p f c", c=2 * D)[:, :, D:2 * D],
                             w2[:, e, :, :]).then_inc(w_raw[e], 16)

            for e in range(EARLY):
                load_raw(e)
            sp.dma_start(xs.rearrange("(a p) c -> a p c", p=BLK),
                         pad_rows.unsqueeze(0).to_broadcast([(SPARE + BLK) // BLK, BLK, PAY])).then_inc(padded, 16)
            sp.dma_start(out[N:N + BLK, :], pad_rows[:, 0:D]).then_inc(out_first, 16)
            sp.wait_ge(early_free, 1)
            for e in range(EARLY, E):
                load_raw(e)
            for t in range(TILES):
                n = ROWS[t]
                sp.wait_ge(h3_ready, t + 1)
                sp.dma_start(out[t * TOK:t * TOK + n, :], h[0:n, t, :]).then_inc(out_first, 16)
            sp.wait_ge(table_ready, 1)
            for b in range(3):
                sp.wait_ge(scattered[b], 32 * (TILES // 3))
            used = blocks_in_use(sp)
            for b in range(NB):
                with used(b):
                    row = sp.value_load(tablei[0:1, T_ROW + b:T_ROW + b + 1], min_val=0, max_val=SPARE)
                    if b >= 2:
                        sp.wait_ge(xt_done, b - 1)
                        sp.wait_ge(gate_ready, b - 1)
                    sp.dma_start(xin[:, b % 2, :], xs[bass.ds(row, BLK), :]).then_inc(xin_ld[b % 2], 16)

        @block.gpsimd
        def _(pool):
            def root(t, rnd):
                n = ROWS[t]
                pool.wait_ge(veps_ready, rnd * TILES + t + 1)
                nc.gpsimd.tensor_tensor(rstd[0:n, t:t + 1], veps[0:n, t:t + 1], nhalf[0:n, :], ALU.pow)\
                    .then_inc(rstd_ready, 1)

            def split_w2(e):
                pool.wait_ge(w2_hi, e + 1)
                hl = we[:, e, W2_HL:WCOLS].rearrange("p (f c) -> p f c", c=2 * D)
                whole = raw[e][:, W2_HL:WCOLS].rearrange("p (f c) -> p f c", c=2 * D)
                nc.gpsimd.tensor_tensor(hl[:, :, D:2 * D], whole[:, :, D:2 * D], hl[:, :, 0:D], ALU.subtract)\
                    .then_inc(lo_pool, 1)

            def split_w1(e):
                pool.wait_ge(w1_hi, e + 1)
                nc.gpsimd.tensor_tensor(we[:, e, A_LO:A_LO + F], raw[e][:, A_LO:A_LO + F], we[:, e, A_HI:A_HI + F],
                                        ALU.subtract)
                nc.gpsimd.tensor_tensor(we[0:DB, e, B_LO:B_LO + F], raw[e][0:DB, B_LO:B_LO + F],
                                        we[0:DB, e, B_HI:B_HI + F], ALU.subtract).then_inc(lo_pool, 1)

            def bias_rows(e0, e1):
                if e1 > EARLY:
                    pool.wait_ge(early_free, 1)
                pool.dma_start(we[DB:DB + 1, e0:e1, B_LO:B_LO + F], b1[e0:e1, :]).then_inc(b1_rows, 16)
                pool.dma_start(we[DB + 1:DB + 2, e0:e1, B_LO:B_LO + F], b1lo_sb[e0:e1, :]).then_inc(b1_rows, 16)

            def dispatch(t):
                n = ROWS[t]
                pool.wait_ge(row_ready, t + 1)
                if t == 0:
                    pool.wait_ge(padded, 16)
                for j in range(2):
                    pool.indirect_dma_start(xs, bass.IndirectOffsetOnAxis(ap=rowu[0:n, t, j:j + 1], axis=0),
                                            pay[0:n, t % 3, :], None).then_inc(scattered[t % 3], 16)

            pool.wait_ge(fixed, 1)
            nc.gpsimd.memset(vp[:, :, :, HD:HD + 1], 1.0).then_inc(ones_ready, 1)
            for t in range(TILES):
                root(t, 0)
            for t in range(TILES):
                n = ROWS[t]
                pool.wait_ge(rope_ready, t + 1)
                nc.gpsimd.tensor_tensor(qk[0:n, t, :], ropec[0:n, t % 2, :], ropes[0:n, t % 2, :], ALU.add)\
                    .then_inc(qk_ready, 1)
                pool.wait_ge(v2_ready, t + 1)
                nc.gpsimd.tensor_tensor(vp[0:n, t, :, PC:VC],
                                        vr[0:n, t % 2, :].rearrange("p (h d) -> p h d", d=HD),
                                        vp[0:n, t, :, HD + 1:PC], ALU.subtract).then_inc(v3_ready, 1)
            pool.wait_ge(b1_lo, 1)
            bias_rows(0, EARLY)
            for i in range(TILES + 1):
                if i >= LAG:
                    root(i - LAG, 1)
                if i >= LAG + 1:
                    dispatch(i - LAG - 1)
                if 1 <= i < EARLY:
                    split_w1(i - 1)
                    split_w2(i - 1)
            root(TILES - 2, 1)
            bias_rows(EARLY, E)
            split_w2(EARLY - 1)
            root(TILES - 1, 1)
            dispatch(TILES - 3)
            dispatch(TILES - 2)
            dispatch(TILES - 1)
            for e in range(EARLY, E):
                split_w2(e)
            pool.wait_ge(out_first, 16 * (TILES + 1))
            used = blocks_in_use(pool)
            for b in range(NB):
                with used(b):
                    pool.wait_ge(y_ready, b + 1)
                    pool.wait_ge(gate_ready, b + 1)
                    pool.indirect_dma_start(out, bass.IndirectOffsetOnAxis(ap=tokblk[:, b:b + 1], axis=0),
                                            y[:, b % 2, :], None, compute_op=ALU.add).then_inc(added, 16)
                    pool.wait_ge(added, 16 * (b + 1))

        @block.tensor
        def _(pe):
            mm = nc.tensor.matmul
            tr = nc.tensor.transpose
            for t in range(TILES):
                n = ROWS[t]
                if t >= 1:
                    pe.wait_ge(ld_x[t], 16)
                for k in range(KC):
                    if t == 0 and k * WPARTS % KC == 0:
                        pe.wait_ge(ld_w[k * WPARTS // KC], 32)
                    mm(bank[t][0:n, 0:D], x_sb[:, t, k, 0:n], wtok_sb[:, k, :], start=(k == 0), stop=False)
                if t == 0:
                    pe.wait_ge(ld_embed, 32)
                mm(bank[t][0:n, 0:D], toksel_sb[:, t * TOK:t * TOK + n], tokrows_sb[:, :], start=False, stop=True)\
                    .then_inc(embed_done, 1)

            def turn(src, bk, n, t):
                tr(bk[0:DA, 0:n], src[0:n, t, 0:DA], ident_sb[0:n, 0:n])
                return tr(bk[0:DB, 128:128 + n], src[0:n, t, DA:D], ident_sb[0:n, 0:n])

            def normal_t(t):
                pe.wait_ge(hn_ready, t + 1)
                pe.wait_ge(h_copied, min(TILES, 5 + t))
                if t >= 2:
                    pe.wait_ge(hnt_copied, t - 1)
                turn(hn, bank[4 + t % 2], ROWS[t], t).then_inc(hnt_done, 1)

            def project(t):
                n, b = ROWS[t], t % 2
                pe.wait_ge(hnt_copied, t + 1)
                if t >= 2:
                    pe.wait_ge(rope_ready, t - 1)
                for j, (a, w) in enumerate(((hnta, wqkva_sb), (hntb, wqkvb_sb))):
                    last = mm(bank[6 + b][0:n, 0:2 * D], a[:, b, 0:n], w[:, 0:2 * D], start=(j == 0), stop=(j == 1))
                last.then_inc(qk_done, 1)
                if t >= 2:
                    pe.wait_ge(vr_ready, t - 1)
                    pe.wait_ge(v1_ready, t - 1)
                for j, (a, w) in enumerate(((hnta, wqkva_sb), (hntb, wqkvb_sb))):
                    last = mm(bank[2 + b][0:n, 0:D], a[:, b, 0:n], w[:, 2 * D:3 * D], start=(j == 0), stop=(j == 1))
                last.then_inc(v_done, 1)

            pe.wait_ge(ld_const, 32)
            pe.wait_ge(ld_attn, ATTN_LOADS)
            normal_t(0)
            for t in range(TILES - 1):
                normal_t(t + 1)
                project(t)

            def qk_t(t):
                n = ROWS[t]
                pe.wait_ge(qk_ready, t + 1)
                if t == 0:
                    pe.wait_ge(rope_ready, TILES - 1)
                else:
                    pe.wait_ge(kbd_ready, t)
                    pe.wait_ge(qt_copied, t)
                for i, c in enumerate((0, D)):
                    tr(bank[6][0:DA, TOK * i:TOK * i + n], qk[0:n, t, c:c + DA], ident_sb[0:n, 0:n])
                    last = tr(bank[6][0:DB, TOK * (2 + i):TOK * (2 + i) + n], qk[0:n, t, c + DA:c + D],
                              ident_sb[0:n, 0:n])
                last.then_inc(qkt_done, 1)

            def scores(t, groups):
                n, b = ROWS[t], t % 2
                pe.wait_ge(kbd_ready, t + 1)
                pe.wait_ge(qt_copied, t + 1)
                for g in groups:
                    if t >= 1:
                        pe.wait_ge(p_ready, GROUPS * (t - 1) + g + 1)
                    elif g == 2:
                        pe.wait_ge(vr_ready, TILES - 1)
                        pe.wait_ge(v1_ready, TILES - 1)
                    q, k = (qta[:, b, 0:n], kbda[:, b, HG * g:HG * g + HG, 0:n]) if g < 2 else \
                           (qtb[:, b, 0:n], kbdb[:, b, :, 0:n])
                    o = bank[g][0:n, 0:HG * TOK].rearrange("p (h s) -> p h s", s=TOK)[:, :, 0:n]
                    mm(o, q, k, start=True, stop=False)
                    mm(o, identh_sb[0:n, 0:n], mask_sb[0:n, 0:n].unsqueeze(1).to_broadcast([n, HG, n]),
                       start=False, stop=True).then_inc(s_done, 1)

            def probs_t(t, groups):
                n, b = ROWS[t], t % 2
                for g in groups:
                    i = GROUPS * t + g
                    pe.wait_ge(p_ready, i + 1)
                    if i >= 2:
                        pe.wait_ge(ptl_ready, i - 1)
                    elif i == 0:
                        pe.wait_ge(vr_ready, TILES)
                        pe.wait_ge(v1_ready, TILES)
                    for j in range(HG):
                        last = tr(bank[3 + i % 2][0:n, TOK * j:TOK * j + n], probs[0:n, b, HG * g + j, 0:n],
                                  ident_sb[0:n, 0:n])
                    last.then_inc(pt_done, 1)

            def values(t, heads):
                n, b = ROWS[t], t % 2
                pe.wait_ge(v3_ready, t + 1)
                if t == 0:
                    pe.wait_ge(ones_ready, 1)
                    pe.wait_ge(rope_ready, TILES)
                else:
                    pe.wait_ge(h2_ready, t)
                for hd in heads:
                    if hd % HG == 0:
                        pe.wait_ge(ptl_ready, GROUPS * t + hd // HG + 1)
                    c = hd * PC
                    mm(bank[7][0:n, c:c + PC], pth[0:n, b, hd, 0:n], vp[0:n, t, hd, 0:PC], start=True, stop=False)
                    mm(bank[7][0:n, c:c + HD], pth[0:n, b, hd, 0:n], vp[0:n, t, hd, PC:VC], start=False, stop=False)
                    last = mm(bank[7][0:n, c:c + PC], ptl[0:n, b, hd, 0:n], vp[0:n, t, hd, 0:PC],
                              start=False, stop=True)
                if hd == HEADS - 1:
                    last.then_inc(pv_done, 1)

            def attended_t(t):
                pe.wait_ge(ao_ready, t + 1)
                b = t % 2
                n = ROWS[t]
                tr(bank[7][0:DA, 0:n], ao[0:n, b, 0:DA], ident_sb[0:n, 0:n])
                tr(bank[7][0:DB, TOK:TOK + n], ao[0:n, b, DA:D], ident_sb[0:n, 0:n]).then_inc(aot_done, 1)

            def out_project(t):
                n, b = ROWS[t], t % 2
                pe.wait_ge(aot_copied, t + 1)
                mm(bank[7][0:n, 2 * TOK:2 * TOK + D], aota[:, b, 0:n], woa_sb[:, :], start=True, stop=False)
                mm(bank[7][0:n, 2 * TOK:2 * TOK + D], aotb[:, b, 0:n], wob_sb[:, :], start=False, stop=True)\
                    .then_inc(wo_done, 1)

            def gates_t(t):
                n = ROWS[t]
                pe.wait_ge(hn_ready, TILES + t + 1)
                if 1 <= t < TILES - 2:
                    pe.wait_ge(h3_ready, t)
                tr(gates_bank[t][0:DA, G0:G0 + n], pay[0:n, t % 3, 0:DA], ident_sb[0:n, 0:n])
                tr(gates_bank[t][0:DB, G1:G1 + n], pay[0:n, t % 3, DA:D], ident_sb[0:n, 0:n]).then_inc(hnt_done, 1)

            def logits(t):
                n, b = ROWS[t], t % 2
                pe.wait_ge(hnt_copied, TILES + t + 1)
                mm(gates_bank[t][0:n, LG:LG + E], hn2ta[:, b, 0:n], wga_sb[:, :], start=True, stop=False)
                mm(gates_bank[t][0:n, LG:LG + E], hn2tb[:, b, 0:n], wgb_sb[:, :], start=False, stop=True)\
                    .then_inc(lg_done, 1)

            def gates_back(t):
                n = ROWS[t]
                pe.wait_ge(comb_ready, t + 1)
                if t >= TILES - 2:
                    pe.wait_ge(row_ready, t + 1)
                tr(gates_bank[t][0:E, CT:CT + n], comb[0:n, t, :], ident_sb[0:n, 0:n]).then_inc(combt_done, 1)

            def ranks(t):
                n = ROWS[t]
                pe.wait_ge(chosen_ready, t + 1)
                if t < TILES - 2:
                    pe.wait_ge(combt_copied, t + 1)
                o = gates_bank[t][0:n, LG:LG + E]
                last = mm(o, before_sb[0:n, 0:n], member[0:n, t, :], start=True, stop=(t == 0))
                for u in range(t):
                    last = mm(o, onesh_sb[0:ROWS[u], 0:n], member[0:ROWS[u], u, :], start=False, stop=(u == t - 1))
                last.then_inc(rank_done, 1)

            def bias2(t):
                n, b = ROWS[t], t % 2
                pe.wait_ge(row_ready, t + 1)
                pe.wait_ge(combt_copied, t + 1)
                mm(gates_bank[t][0:n, 0:D], combt[:, t % 3, 0:n], b2_sb[:, :], start=True, stop=True)\
                    .then_inc(bias_done, 1)

            pe.wait_ge(ld_rest, REST_LOADS)
            qk_t(0)
            project(TILES - 1)
            for i in range(TILES + 1):
                if i >= 1:
                    probs_t(i - 1, (0, 1))
                if i >= 2:
                    attended_t(i - 2)
                if i + 1 < TILES:
                    qk_t(i + 1)
                if i < TILES:
                    scores(i, (0,))
                if i >= LAG + 1:
                    gates_back(i - LAG - 1)
                if i >= 1:
                    probs_t(i - 1, (2,))
                if i >= LAG + 1:
                    ranks(i - LAG - 1)
                if i < TILES:
                    scores(i, (1,))
                if i >= 2:
                    out_project(i - 2)
                if i < TILES:
                    scores(i, (2,))
                if i >= LAG + 1:
                    bias2(i - LAG - 1)
                if i >= 1:
                    values(i - 1, range(HEADS // 2))
                if i >= LAG:
                    gates_t(i - LAG)
                if i >= 1:
                    values(i - 1, range(HEADS // 2, HEADS))
                if i >= LAG:
                    logits(i - LAG)
            attended_t(TILES - 1)
            out_project(TILES - 1)
            gates_t(TILES - 2)
            logits(TILES - 2)
            gates_back(TILES - 3)
            ranks(TILES - 3)
            gates_t(TILES - 1)
            ranks(TILES - 2)
            logits(TILES - 1)
            gates_back(TILES - 2)
            ranks(TILES - 1)
            for t in range(TILES):
                last = mm(bank[0][:, 0:E], onesh_sb[0:ROWS[t], :], member[0:ROWS[t], t, :],
                          start=(t == 0), stop=(t == TILES - 1))
            last.then_inc(count_done, 1)
            gates_back(TILES - 1)
            for t in range(TILES - 3, TILES):
                bias2(t)

            pe.wait_ge(table_ready, 1)

            def block_t(b):
                pe.wait_ge(xin_ld[b % 2], 16 * (b // 2 + 1))
                if b >= 1:
                    pe.wait_ge(xlo_ready, b)
                tr(bank[0][:, 0:BLK], xin[:, b % 2, 0:DA], ident_sb[:, :])
                tr(bank[0][:, BLK:2 * BLK], xin[:, b % 2, DA:2 * DA], ident_sb[:, :]).then_inc(xt_done, 1)

            def layer1(b, expert):
                pe.wait_ge(xlo_ready, b + 1)
                for hf in range(2):
                    if b >= 1:
                        pe.wait_ge(gelu_done, 2 * b - 1 + hf)
                    parts = ((xahi, A_HI), (xalo, A_HI), (xahi, A_LO), (xb1, B_HI), (xb2, B_LO))
                    for i, (x, c) in enumerate(parts):
                        rows = x.shape[0]
                        w = we[0:rows, bass.ds(expert, 1), c + hf * FH:c + hf * FH + FH].rearrange("p e c -> p (e c)")
                        last = mm(bank[1 + hf][:, 0:FH], x[:, :], w, start=(i == 0), stop=(i == 4))
                    last.then_inc(l1_done, 1)

            def hidden_t(b):
                for q, (f0, f1) in enumerate(((0, 4), (4, FC))):
                    pe.wait_ge(gelu_done, 2 * b + 2)
                    if b >= 1:
                        pe.wait_ge(htlo_ready, 2 * b - 1 + q)
                    for f in range(f0, f1):
                        last = tr(bank[3 + q][:, (f - f0) * 128:(f - f0) * 128 + 128], hid[:, f * 128:f * 128 + 128],
                                  ident_sb[:, :])
                    last.then_inc(ht_done, 1)

            def layer2(b, expert):
                if b >= 2:
                    pe.wait_ge(y_ready, b - 1)
                o = bank[6 + b % 2]
                for f in range(FC):
                    if f in (0, 4):
                        pe.wait_ge(htlo_ready, 2 * b + 1 + (f == 4))
                    c = W2_HL + f * 2 * D
                    w = we[:, bass.ds(expert, 1), c:c + 2 * D].rearrange("p e c -> p (e c)")
                    mm(o[:, 0:2 * D], hthi[:, f, :], w, start=(f == 0), stop=False)
                    w = we[:, bass.ds(expert, 1), c:c + D].rearrange("p e c -> p (e c)")
                    last = mm(o[:, 0:D], htlo[:, f, :], w, start=False, stop=(f == FC - 1))
                last.then_inc(l2_done, 1)

            def expert_of(b):
                return pe.value_load(tablei[0:1, T_EXP + b:T_EXP + b + 1], min_val=0, max_val=E - 1)

            pe.wait_ge(w1_hi, 1)
            for _ in range(BLOCK_WARM_UP):
                mm(bank[3][:, 0:FH], we[:, 0, A_HI:A_HI + 128], we[:, 0, A_HI:A_HI + FH], start=True, stop=True)
            pe.wait_ge(early_free, 1)
            block_t(0)
            pe.wait_ge(lo_dve, E - EARLY + 1)
            pe.wait_ge(lo_pool, E + EARLY - 1)
            pe.wait_ge(b1_rows, 64)
            expert = expert_of(0)
            layer1(0, expert)
            block_t(1)
            used = blocks_in_use(pe)
            for b in range(NB):
                following = expert_of(b + 1) if b + 1 < NB else None
                with used(b):
                    hidden_t(b)
                    if b + 1 < NB:
                        with used(b + 1):
                            layer1(b + 1, following)
                            if b + 2 < NB:
                                with used(b + 2):
                                    block_t(b + 2)
                    layer2(b, expert)
                expert = following

        @block.scalar
        def _(act):
            fn = nc.scalar.activation

            def copy_normal_t(t, da, dbuf, rnd, bk, c0, c1):
                n = ROWS[t]
                act.wait_ge(hnt_done, rnd * TILES + t + 1)
                fn(da, bk[0:DA, c0:c0 + n], ACT.Copy)
                fn(dbuf, bk[0:DB, c1:c1 + n], ACT.Copy).then_inc(hnt_copied, 1)

            for t in range(TILES):
                n = ROWS[t]
                act.wait_ge(embed_done, t + 1)
                fn(h[0:n, t, :], bank[t][0:n, 0:D], ACT.Copy).then_inc(h_copied, 1)

            def first_t(t):
                if t == 0:
                    act.wait_ge(embed_done, TILES)
                if t >= 2:
                    act.wait_ge(v_done, t - 1)
                copy_normal_t(t, hnta[:, t % 2, 0:ROWS[t]], hntb[:, t % 2, 0:ROWS[t]], 0, bank[4 + t % 2],
                              0, 128)

            def v_parts(t):
                n, b = ROWS[t], t % 2
                act.wait_ge(v_done, t + 1)
                fn(vp[0:n, t, :, 0:HD], bank[2 + b][0:n, 0:D].rearrange("p (h d) -> p h d", d=HD), ACT.Copy)\
                    .then_inc(v1_ready, 1)
                act.wait_ge(vr_ready, t + 1)
                fn(vp[0:n, t, :, HD + 1:PC], vr[0:n, b, :].rearrange("p (h d) -> p h d", d=HD), ACT.Copy)\
                    .then_inc(v2_ready, 1)

            first_t(0)
            for t in range(TILES - 1):
                first_t(t + 1)
                v_parts(t)

            def copy_q(t):
                n, b = ROWS[t], t % 2
                act.wait_ge(qkt_done, t + 1)
                if t >= 2:
                    act.wait_ge(s_done, GROUPS * (t - 1))
                fn(qta[:, b, 0:n], bank[6][0:DA, 0:n], ACT.Copy)
                fn(qtb[:, b, 0:n], bank[6][0:DB, 2 * TOK:2 * TOK + n], ACT.Copy).then_inc(qt_copied, 1)

            def exps(t, g):
                n, b = ROWS[t], t % 2
                act.wait_ge(max_ready, GROUPS * t + g + 1)
                if t >= 2:
                    act.wait_ge(pt_done, GROUPS * (t - 2) + g + 1)
                elif t == 0 and g == 0:
                    act.wait_ge(qk_ready, TILES)
                    act.wait_ge(v3_ready, TILES)
                    act.wait_ge(v_done, TILES)
                for j in range(HG):
                    hd = HG * g + j
                    last = fn(probs[0:n, b, hd, 0:n], bank[g][0:n, TOK * j:TOK * j + n], ACT.Exp,
                              bias=sneg[0:n, b, hd:hd + 1], scale=float(HD) ** -0.5)
                last.then_inc(p_ready, 1)

            def high(t, g):
                n, b = ROWS[t], t % 2
                i = GROUPS * t + g
                act.wait_ge(pt_done, i + 1)
                if t >= 2:
                    act.wait_ge(pv_done, t - 1)
                fn(pth[0:n, b, HG * g:HG * g + HG, 0:n],
                   bank[3 + i % 2][0:n, 0:HG * TOK].rearrange("p (h s) -> p h s", s=TOK)[:, :, 0:n], ACT.Copy)\
                    .then_inc(pth_ready, 1)

            def copy_attended(t):
                n, b = ROWS[t], t % 2
                act.wait_ge(aot_done, t + 1)
                if t >= 2:
                    act.wait_ge(wo_done, t - 1)
                fn(aota[:, b, 0:n], bank[7][0:DA, 0:n], ACT.Copy)
                fn(aotb[:, b, 0:n], bank[7][0:DB, TOK:TOK + n], ACT.Copy).then_inc(aot_copied, 1)

            def copy_second(t):
                n, b = ROWS[t], t % 2
                if t >= 2:
                    act.wait_ge(lg_done, t - 1)
                copy_normal_t(t, hn2ta[:, b, 0:n], hn2tb[0:DB, b, 0:n], 1, gates_bank[t], G0, G1)

            def gate_exp(t):
                n = ROWS[t]
                act.wait_ge(gneg_ready, t + 1)
                fn(gexp[0:n, t, :], gmax[0:n, t, :], ACT.Exp, bias=gneg[0:n, t:t + 1],
                   accum_out=gsum[0:n, t:t + 1]).then_inc(gexp_ready, 1)

            def copy_gates(t):
                n, b = ROWS[t], t % 2
                act.wait_ge(combt_done, t + 1)
                if t >= 3:
                    act.wait_ge(bias_done, t - 2)
                fn(combt[:, t % 3, 0:n], gates_bank[t][0:E, CT:CT + n], ACT.Copy).then_inc(combt_copied, 1)

            def round_w1(e):
                act.wait_ge(w_raw[e], 64)
                fn(we[:, e, A_HI:A_HI + F], raw[e][:, A_LO:A_LO + F], ACT.Copy)
                fn(we[:, e, B_HI:B_HI + F], raw[e][:, B_HI:B_HI + F], ACT.Copy).then_inc(w1_hi, 1)

            def round_w2(e):
                act.wait_ge(w_raw[e], 64)
                hl = we[:, e, W2_HL:WCOLS].rearrange("p (f c) -> p f c", c=2 * D)
                whole = raw[e][:, W2_HL:WCOLS].rearrange("p (f c) -> p f c", c=2 * D)
                fn(hl[:, :, 0:D], whole[:, :, D:2 * D], ACT.Copy).then_inc(w2_hi, 1)

            copy_q(0)
            v_parts(TILES - 1)
            for i in range(TILES + 1):
                if i >= 1:
                    high(i - 1, 0)
                    high(i - 1, 1)
                if i >= 2:
                    copy_attended(i - 2)
                if i + 1 < TILES:
                    copy_q(i + 1)
                if i >= LAG + 1:
                    copy_gates(i - LAG - 1)
                if i < EARLY:
                    round_w1(i)
                if i >= 1:
                    high(i - 1, 2)
                if i < TILES:
                    exps(i, 0)
                if 1 <= i < EARLY:
                    round_w2(i)
                if i < TILES:
                    exps(i, 1)
                if i >= LAG:
                    copy_second(i - LAG)
                if i < TILES:
                    exps(i, 2)
                if i == 0:
                    round_w2(i)
                if LAG <= i < TILES:
                    gate_exp(i - LAG)
            copy_attended(TILES - 1)
            copy_second(TILES - 2)
            gate_exp(TILES - 3)
            copy_gates(TILES - 3)
            gate_exp(TILES - 2)
            copy_second(TILES - 1)
            round_w2(EARLY)
            copy_gates(TILES - 2)
            gate_exp(TILES - 1)
            copy_gates(TILES - 1)
            round_w1(EARLY)
            for e in range(EARLY + 1, E):
                round_w1(e)
                round_w2(e)

            def tokens_high(b):
                act.wait_ge(xt_done, b + 1)
                if b >= 1:
                    act.wait_ge(l1_done, 2 * b)
                fn(xahi[:, :], bank[0][:, 0:BLK], ACT.Copy)
                fn(xb1[:, :], bank[0][:, BLK:2 * BLK], ACT.Copy)
                fn(xb2[0:DB, :], bank[0][0:DB, BLK:2 * BLK], ACT.Copy).then_inc(xhi_ready, 1)

            def gelu(b, halves=(0, 1)):
                for hf in halves:
                    act.wait_ge(l1_done, 2 * b + hf + 1)
                    if b >= 1:
                        act.wait_ge(ht_done, 2 * b)
                    else:
                        act.wait_ge(table_ready, 1)
                    fn(hid[:, hf * FH:hf * FH + FH], bank[1 + hf][:, 0:FH], ACT.Gelu).then_inc(gelu_done, 1)

            def hidden_high(b):
                for q, (f0, f1) in enumerate(((0, 4), (4, FC))):
                    act.wait_ge(ht_done, 2 * b + q + 1)
                    if b >= 1:
                        act.wait_ge(l2_done, b)
                    fn(hthi[:, f0:f1, :], bank[3 + q][:, 0:(f1 - f0) * 128].rearrange("p (f s) -> p f s", s=128),
                       ACT.Copy).then_inc(hthi_ready, 1)

            def output_cross(b):
                act.wait_ge(l2_done, b + 1)
                act.wait_ge(gate_ready, b + 1)
                if b >= 1:
                    act.wait_ge(y_ready, b)
                fn(y1[:, :], bank[6 + b % 2][:, D:2 * D], ACT.Copy, scale=gblk[:, b:b + 1]).then_inc(y1_ready, 1)

            fn(preload[:, :], nhalf[:, :], ACT.Gelu)
            tokens_high(0)
            gelu(0, (0,))
            tokens_high(1)
            gelu(0, (1,))
            used = blocks_in_use(act)
            for b in range(NB):
                with used(b):
                    hidden_high(b)
                    if b + 1 < NB:
                        with used(b + 1):
                            gelu(b + 1)
                            if b + 2 < NB:
                                with used(b + 2):
                                    tokens_high(b + 2)
                    output_cross(b)

        @block.vector
        def _(dve):
            v = nc.vector
            steps = [0]

            def step(ins):
                steps[0] += 1
                ins.then_inc(dve_step, 1)
                dve.wait_ge(dve_step, steps[0])

            def norm_stats(t):
                n = ROWS[t]
                step(v.bn_stats(stats[0:n, t, :], h[0:n, t, :]))
                step(v.bn_aggr(mv[0:n, t, :], stats[0:n, t, :]))
                v.tensor_scalar(veps[0:n, t:t + 1], mv[0:n, t, 1:2], EPS, None, ALU.add).then_inc(veps_ready, 1)

            def norm_apply(t, rnd):
                n = ROWS[t]
                c = slice(t, t + 1)
                dve.wait_ge(rstd_ready, rnd * TILES + t + 1)
                if rnd == 0:
                    v.tensor_scalar(hn[0:n, t, :], h[0:n, t, :], mv[0:n, t, 0:1], rstd[0:n, c], ALU.subtract,
                                    ALU.mult).then_inc(hn_ready, 1)
                    return
                if t >= 3:
                    dve.wait_ge(scattered[t % 3], 32 * (t // 3))
                v.tensor_scalar(pay[0:n, t % 3, 0:D], h[0:n, t, :], mv[0:n, t, 0:1], rstd[0:n, c], ALU.subtract,
                                ALU.mult)
                v.tensor_copy(pay[0:n, t % 3, C_TOK:C_TOK + 1].bitcast(U32), tokids_sb[0:n, t:t + 1])
                v.tensor_scalar(pay[0:n, t % 3, D:D + DB], h[0:n, t, DA:D], mv[0:n, t, 0:1], rstd[0:n, c],
                                ALU.subtract, ALU.mult).then_inc(hn_ready, 1)

            v.memset(nhalf[:, :], -0.5).then_inc(fixed, 1)
            v.memset(hn2tb[DB:DB + 1, :, :], 1.0).then_inc(fixed, 1)

            def split_w1(e):
                dve.wait_ge(w1_hi, e + 1)
                v.tensor_tensor(we[:, e, A_LO:A_LO + F], raw[e][:, A_LO:A_LO + F], we[:, e, A_HI:A_HI + F],
                                ALU.subtract)
                v.tensor_tensor(we[0:DB, e, B_LO:B_LO + F], raw[e][0:DB, B_LO:B_LO + F],
                                we[0:DB, e, B_HI:B_HI + F], ALU.subtract).then_inc(lo_dve, 1)

            for t in range(TILES + 1):
                if t < TILES:
                    dve.wait_ge(h_copied, t + 1)
                    norm_stats(t)
                if t >= 1:
                    norm_apply(t - 1, 0)

            dve.wait_ge(b1_raw, 16)
            step(v.tensor_copy(b1hi_sb[:, :], b1raw_sb[:, :]))
            v.tensor_tensor(b1lo_sb[:, :], b1raw_sb[:, :], b1hi_sb[:, :], ALU.subtract).then_inc(b1_lo, 1)

            def rope(t):
                n, b = ROWS[t], t % 2
                dve.wait_ge(qk_done, t + 1)
                if t >= 2:
                    dve.wait_ge(qk_ready, t - 1)
                x = bank[6 + b][0:n, 0:2 * D].rearrange("p (a c) -> p a c", a=2)
                v.tensor_tensor(ropec[0:n, b, :].rearrange("p (a c) -> p a c", a=2), x,
                                cos_sb[0:n, :].unsqueeze(1).to_broadcast([n, 2, D]), ALU.mult)
                x = bank[6 + b][0:n, 0:2 * D].rearrange("p (c s) -> p c s", s=2)
                turned = ropes[0:n, b, :].rearrange("p (c s) -> p c s", s=2)
                sn = sin_sb[0:n, :].rearrange("p (c s) -> p c s", s=2)
                for a in range(2):
                    for s in range(2):
                        cs = slice(a * D // 2, (a + 1) * D // 2)
                        last = v.tensor_tensor(turned[:, cs, s], x[:, cs, 1 - s], sn[:, :, s], ALU.mult)
                last.then_inc(rope_ready, 1)
                dve.wait_ge(v_done, t + 1)
                dve.wait_ge(v1_ready, t + 1)
                if t >= 2:
                    dve.wait_ge(v3_ready, t - 1)
                v.tensor_tensor(vr[0:n, b, :].rearrange("p (h d) -> p h d", d=HD),
                                bank[2 + b][0:n, 0:D].rearrange("p (h d) -> p h d", d=HD),
                                vp[0:n, t, :, 0:HD], ALU.subtract).then_inc(vr_ready, 1)

            def spread_k(t):
                n, b = ROWS[t], t % 2
                if t == 0:
                    dve.wait_ge(hnt_done, TILES)
                dve.wait_ge(qkt_done, t + 1)
                dve.wait_ge(qt_copied, t + 1)
                if t >= 2:
                    dve.wait_ge(s_done, GROUPS * (t - 1))
                v.tensor_tensor(kbda[:, b, :, 0:n], bank[6][0:DA, TOK:TOK + n].unsqueeze(1).to_broadcast([DA, 8, n]),
                                headmask_sb[0:DA, :].unsqueeze(2).to_broadcast([DA, 8, n]), ALU.mult)
                v.tensor_tensor(kbdb[:, b, :, 0:n],
                                bank[6][0:DB, 3 * TOK:3 * TOK + n].unsqueeze(1).to_broadcast([DB, 4, n]),
                                headmask_sb[0:DB, 0:4].unsqueeze(2).to_broadcast([DB, 4, n]), ALU.mult)\
                    .then_inc(kbd_ready, 1)

            def scores_max(t, groups):
                n, b = ROWS[t], t % 2
                for g in groups:
                    hs = slice(HG * g, HG * g + HG)
                    dve.wait_ge(s_done, GROUPS * t + g + 1)
                    if t >= 2:
                        dve.wait_ge(p_ready, GROUPS * (t - 2) + g + 1)
                    s = bank[g][0:n, 0:HG * TOK].rearrange("p (h s) -> p h s", s=TOK)[:, :, 0:n]
                    step(v.tensor_reduce(smax[0:n, b, hs], s, AX.X, ALU.max))
                    v.tensor_scalar(sneg[0:n, b, hs], smax[0:n, b, hs], -float(HD) ** -0.5, None, ALU.mult)\
                        .then_inc(max_ready, 1)

            def low(t, groups):
                n, b = ROWS[t], t % 2
                for g in groups:
                    i = GROUPS * t + g
                    hs = slice(HG * g, HG * g + HG)
                    dve.wait_ge(pth_ready, i + 1)
                    if t >= 2:
                        dve.wait_ge(pv_done, t - 1)
                    v.tensor_tensor(ptl[0:n, b, hs, 0:n],
                                    bank[3 + i % 2][0:n, 0:HG * TOK].rearrange("p (h s) -> p h s", s=TOK)[:, :, 0:n],
                                    pth[0:n, b, hs, 0:n], ALU.subtract).then_inc(ptl_ready, 1)

            def norm_out(t):
                n, b = ROWS[t], t % 2
                dve.wait_ge(pv_done, t + 1)
                if t >= 2:
                    dve.wait_ge(aot_done, t - 1)
                o = bank[7][0:n, 0:HEADS * PC].rearrange("p (h d) -> p h d", d=PC)
                a = ao[0:n, b, :].rearrange("p (h d) -> p h d", d=HD)
                v.reciprocal(rsum[0:n, b, :], o[:, :, HD])
                step(v.tensor_copy(a, o[:, :, 0:HD]))
                step(v.tensor_tensor(a, o[:, :, HD + 1:PC], a, ALU.add))
                v.tensor_tensor(a, a,
                                rsum[0:n, b, :].unsqueeze(2).to_broadcast([n, HEADS, HD]), ALU.mult)\
                    .then_inc(ao_ready, 1)

            def residual(t):
                n = ROWS[t]
                dve.wait_ge(wo_done, t + 1)
                v.tensor_tensor(h[0:n, t, :], bank[7][0:n, 2 * TOK:2 * TOK + D], h[0:n, t, :], ALU.add)\
                    .then_inc(h2_ready, 1)

            def second_stats(t):
                dve.wait_ge(h2_ready, t + 1)
                norm_stats(t)

            def choose(t):
                n, b = ROWS[t], t % 2
                lg = gates_bank[t][0:n, LG:LG + E]
                dve.wait_ge(lg_done, t + 1)
                step(v.max(gmax[0:n, t, :], lg))
                v.tensor_scalar(gneg[0:n, t:t + 1], gmax[0:n, t, 0:1], -1.0, None, ALU.mult).then_inc(gneg_ready, 1)
                step(v.max_index(gidx[0:n, t, :], gmax[0:n, t, :], lg))
                step(v.tensor_copy(pay[0:n, t % 3, C_IDX:C_IDX + 2], gidx[0:n, t, 0:2]))
                for j in range(2):
                    last = v.tensor_scalar(chosen[0:n, t, j, :], iota_sb[0:n, :],
                                           pay[0:n, t % 3, C_IDX + j:C_IDX + j + 1], None, ALU.is_equal)
                step(last)
                v.tensor_tensor(member[0:n, t, :], chosen[0:n, t, 0, :], chosen[0:n, t, 1, :], ALU.add)\
                    .then_inc(chosen_ready, 1)
                dve.wait_ge(gexp_ready, t + 1)
                step(v.reciprocal(grec[0:n, t:t + 1], gsum[0:n, t:t + 1]))
                step(v.tensor_scalar(pay[0:n, t % 3, C_GATE:C_GATE + 2], gexp[0:n, t, 0:2], grec[0:n, t:t + 1], None,
                                     ALU.mult))
                for j in range(2):
                    last = v.tensor_scalar(comb2[0:n, b, j, :], chosen[0:n, t, j, :],
                                           pay[0:n, t % 3, C_GATE + j:C_GATE + j + 1], None, ALU.mult)
                step(last)
                v.tensor_tensor(comb[0:n, t, :], comb2[0:n, b, 0, :], comb2[0:n, b, 1, :], ALU.add)\
                    .then_inc(comb_ready, 1)

            def rows(t):
                n, b = ROWS[t], t % 2
                dve.wait_ge(rank_done, t + 1)
                step(v.tensor_tensor(rowof[0:n, t, :], gates_bank[t][0:n, LG:LG + E], rowbase_sb[0:n, :], ALU.add))
                step(v.tensor_tensor(rowsel[0:n, b, :, :], chosen[0:n, t, :, :],
                                     rowof[0:n, t, :].unsqueeze(1).to_broadcast([n, 2, E]), ALU.mult))
                step(v.tensor_reduce(rowf[0:n, t, :], rowsel[0:n, b, :, :], AX.X, ALU.add))
                v.tensor_copy(rowu[0:n, t, :], rowf[0:n, t, :]).then_inc(row_ready, 1)

            def add_bias2(t):
                n = ROWS[t]
                dve.wait_ge(bias_done, t + 1)
                v.tensor_tensor(h[0:n, t, :], gates_bank[t][0:n, 0:D], h[0:n, t, :], ALU.add).then_inc(h3_ready, 1)

            dve.wait_ge(ld_attn, ATTN_LOADS)
            for t in range(TILES - 1):
                rope(t)
            spread_k(0)
            rope(TILES - 1)
            for i in range(TILES + 1):
                if i >= 1:
                    low(i - 1, (0, 1))
                if i >= LAG:
                    second_stats(i - LAG)
                if i + 1 < TILES:
                    spread_k(i + 1)
                if i < TILES:
                    scores_max(i, (0,))
                if i >= LAG:
                    norm_apply(i - LAG, 1)
                if i >= 1:
                    low(i - 1, (2,))
                if i >= LAG + 1:
                    rows(i - LAG - 1)
                if i >= 2:
                    residual(i - 2)
                if i < TILES:
                    scores_max(i, (1,))
                if i >= LAG + 1:
                    add_bias2(i - LAG - 1)
                if i < TILES:
                    scores_max(i, (2,))
                if i >= 1:
                    norm_out(i - 1)
                if i == TILES:
                    v.memset(xb2[DB:DB + 2, :].bitcast(F32), 1.0).then_inc(early_free, 1)
                    second_stats(TILES - 2)
                    norm_apply(TILES - 2, 1)
                if i >= LAG:
                    choose(i - LAG)
            residual(TILES - 1)
            second_stats(TILES - 1)
            rows(TILES - 3)
            norm_apply(TILES - 1, 1)
            choose(TILES - 2)
            rows(TILES - 2)
            choose(TILES - 1)
            rows(TILES - 1)

            dve.wait_ge(count_done, 1)
            step(v.tensor_tensor(over[:, :, :], bank[0][:, 0:E].unsqueeze(2).to_broadcast([128, E, MAXB]),
                                 steps_sb[:, :].unsqueeze(1).to_broadcast([128, E, MAXB]), ALU.is_gt))
            step(v.tensor_reduce(blocks[:, :], over[:, :, :], AX.X, ALU.add))
            v.tensor_scalar(rest[:, :], blocks[:, :], -float(BLK), float(CAP), ALU.mult, ALU.add)
            step(v.tensor_tensor(blocks8[:, :, :], lower8_sb[:, :, :],
                                 blocks[:, :].unsqueeze(1).to_broadcast([128, E, E]), ALU.mult))
            step(v.tensor_reduce(ends[:, :], blocks8[:, :, :], AX.X, ALU.add))
            step(v.tensor_tensor(passed[:, 0, :, :], blockids_sb[:, :].unsqueeze(2).to_broadcast([128, NB, E]),
                                 ends[:, :].unsqueeze(1).to_broadcast([128, NB, E]), ALU.is_ge))
            step(v.tensor_tensor(passed[:, 1, :, :], passed[:, 0, :, :],
                                 rest[:, :].unsqueeze(1).to_broadcast([128, NB, E]), ALU.mult))
            step(v.tensor_reduce(tmp_nb[:, :, :], passed[:, :, :, :], AX.X, ALU.add))
            step(v.scalar_tensor_tensor(out=tmp_nb[:, 1, :], in0=blockids_sb[:, :], scalar=float(BLK),
                                        in1=tmp_nb[:, 1, :], op0=ALU.mult, op1=ALU.add))
            v.tensor_scalar(table[:, :], tmp_nb[:, 0, :], float(E - 1), None, ALU.min)
            v.tensor_copy(tablei[:, T_LIVE:T_LIVE + 1], ends[:, E - 1:E])
            v.tensor_scalar(tablei[:, T_EXP:T_EXP + NB], tmp_nb[:, 0, :], float(E - 1), None, ALU.min)
            v.tensor_scalar(tablei[:, T_ROW:T_ROW + NB], tmp_nb[:, 1, :], float(SPARE), None, ALU.min)\
                .then_inc(table_ready, 1)

            for t in range(TILES - 3, TILES):
                add_bias2(t)

            for e in range(EARLY - 1, E):
                split_w1(e)

            def tokens_low(b):
                dve.wait_ge(xhi_ready, b + 1)
                v.tensor_tensor(xalo[:, :], bank[0][:, 0:BLK], xahi[:, :], ALU.subtract)
                v.tensor_tensor(xb1[DB:128, :], bank[0][DB:128, BLK:2 * BLK], xb1[DB:128, :], ALU.subtract)\
                    .then_inc(xlo_ready, 1)

            def block_gates(b):
                x = xin[:, b % 2, :]
                dve.wait_ge(xin_ld[b % 2], 16 * (b // 2 + 1))
                v.tensor_copy(tokblk[:, b:b + 1], x[:, C_TOK:C_TOK + 1].bitcast(U32))
                step(v.scalar_tensor_tensor(out=gsel[:, b % 2, :], in0=x[:, C_IDX:C_IDX + 2],
                                            scalar=table[:, b:b + 1], in1=x[:, C_GATE:C_GATE + 2],
                                            op0=ALU.is_equal, op1=ALU.mult))
                v.tensor_tensor(gblk[:, b:b + 1], gsel[:, b % 2, 0:1], gsel[:, b % 2, 1:2], ALU.add)\
                    .then_inc(gate_ready, 1)

            def hidden_low(b):
                for q, (f0, f1) in enumerate(((0, 4), (4, FC))):
                    dve.wait_ge(hthi_ready, 2 * b + q + 1)
                    v.tensor_tensor(htlo[:, f0:f1, :],
                                    bank[3 + q][:, 0:(f1 - f0) * 128].rearrange("p (f s) -> p f s", s=128),
                                    hthi[:, f0:f1, :], ALU.subtract).then_inc(htlo_ready, 1)

            def output(b):
                dve.wait_ge(y1_ready, b + 1)
                if b >= 2:
                    dve.wait_ge(added, 16 * (b - 1))
                v.scalar_tensor_tensor(out=y[:, b % 2, :], in0=bank[6 + b % 2][:, 0:D], scalar=gblk[:, b:b + 1],
                                       in1=y1[:, :], op0=ALU.mult, op1=ALU.add).then_inc(y_ready, 1)

            block_gates(0)
            tokens_low(0)
            block_gates(1)
            tokens_low(1)
            used = blocks_in_use(dve)
            for b in range(NB):
                with used(b):
                    hidden_low(b)
                    if b + 2 < NB:
                        with used(b + 2):
                            block_gates(b + 2)
                            tokens_low(b + 2)
                    output(b)


def constants():
    import numpy as np
    bf16 = mybir.dt.np(BF16)
    i = np.arange(D // 2, dtype=np.float64)
    theta = 10000.0 ** (-2.0 * i / D)
    m_theta = np.repeat(np.arange(1, SEQ + 1, dtype=np.float64)[:, None] * theta[None, :], 2, axis=-1)
    pos = np.arange(TOK) % SEQ
    sign = np.where(np.arange(D) % 2 == 0, -1.0, 1.0)
    img = np.arange(TOK) // SEQ
    allowed = (img[:, None] == img[None, :]) & (pos[None, :] <= pos[:, None])
    tok = np.arange(N)
    pad = np.zeros((BLK, PAY), np.float32)
    pad[:, C_TOK] = np.arange(N, N + BLK, dtype=np.uint32).view(np.float32)
    return {
        "tok_sel": np.stack([tok % SEQ != 0, tok % SEQ == 0]).astype(np.float32),
        "rope_cos": np.cos(m_theta).astype(np.float32)[pos],
        "rope_sin": (np.sin(m_theta).astype(np.float32)[pos] * sign).astype(np.float32),
        "mask": np.where(allowed, 0.0, -1e30).astype(bf16),
        "ident": np.eye(128, dtype=np.float32),
        "ident_half": np.eye(128, dtype=np.float32).astype(bf16),
        "head_mask": (np.arange(128)[:, None] // HD == np.arange(8)[None, :]).astype(np.float32),
        "iota8": np.tile(np.arange(E, dtype=np.float32), (128, 1)),
        "before": (np.arange(TOK)[:, None] < np.arange(TOK)[None, :]).astype(np.float32).astype(bf16),
        "ones_half": np.ones((TOK, 128), np.float32).astype(bf16),
        "tok_ids": (np.arange(TILES)[None, :] * TOK + np.arange(TOK)[:, None]).astype(np.uint32),
        "pad_rows": pad,
        "row_base": np.tile(CAP * np.arange(E, dtype=np.float32), (128, 1)),
        "block_steps": np.tile(BLK * np.arange(MAXB, dtype=np.float32), (128, 1)),
        "lower8": np.tile(np.tril(np.ones((E, E), np.float32))[None], (128, 1, 1)),
        "block_ids": np.tile(np.arange(NB, dtype=np.float32), (128, 1)),
    }


def laid_out(x, cls_tok, L0_tok_W, L0_tok_b, L0_attn_W_q, L0_attn_W_k, L0_attn_W_v, L0_attn_W_o, L0_ffn_Wg,
             L0_ffn_bg, L0_ffn_W1, L0_ffn_b1, L0_ffn_W2, L0_ffn_b2):
    import numpy as np
    a = [np.asarray(v) for v in (x, cls_tok, L0_tok_W, L0_tok_b, L0_attn_W_q, L0_attn_W_k, L0_attn_W_v, L0_attn_W_o,
                                 L0_ffn_Wg, L0_ffn_bg, L0_ffn_W1, L0_ffn_b1, L0_ffn_W2, L0_ffn_b2)]
    x, cls_tok, wt, bt, wq, wk, wv, wo, wg, bg, w1, b1, w2, b2 = a
    p = 16
    g = x.shape[2] // p
    cols = np.zeros((TILES * TOK, KC * 128), x.dtype).reshape(TILES * TOK, -1)
    body = x.reshape(IMAGES, 3, g, p, g, p).transpose(0, 2, 4, 1, 3, 5).reshape(IMAGES, g * g, -1)
    cols[:N].reshape(IMAGES, SEQ, -1)[:, 1:] = body
    wqkv = np.concatenate([wq.T, wk.T, wv.T], axis=1)
    return {
        "patches": cols.reshape(TILES, TOK, KC, 128).transpose(0, 3, 2, 1),
        "w_tok": wt.reshape(D, KC, 128).transpose(2, 1, 0),
        "tok_rows": np.stack([bt, cls_tok.reshape(D)]),
        "w_qkv_a": wqkv[:DA], "w_qkv_b": wqkv[DA:],
        "w_o_a": wo.T[:DA], "w_o_b": wo.T[DA:],
        "w_g_a": wg[:DA], "w_g_b": np.concatenate([wg[DA:], bg[None]]),
        "w1_a": w1[:, :DA].transpose(1, 0, 2), "w1_b": w1[:, DA:].transpose(1, 0, 2),
        "w1_bb": np.concatenate([w1[:, DA:], w1[:, DA:]], axis=1).transpose(1, 0, 2),
        "b1": b1,
        "w2": w2.reshape(E, FC, 128, D).transpose(2, 0, 1, 3),
        "b2": b2,
    }


_INS = ["patches", "w_tok", "tok_rows", "tok_sel", "w_qkv_a", "w_qkv_b", "rope_cos", "rope_sin", "mask", "ident",
        "ident_half", "head_mask", "w_o_a", "w_o_b", "w_g_a", "w_g_b", "iota8", "w1_a", "w1_bb", "w1_b", "b1", "w2",
        "b2", "before", "ones_half", "tok_ids", "pad_rows", "row_base", "block_steps", "lower8", "block_ids"]


def kernel(**inputs):
    import numpy as np
    import concourse.bacc as bacc
    from concourse.bass_utils import run_bass_kernel_spmd

    nc = bacc.Bacc("TRN2", target_bir_lowering=False, num_devices=1)
    given = {**constants(), **laid_out(**inputs)}
    arrays, args = {}, []
    for name in _INS:
        a = np.ascontiguousarray(given[name])
        arrays[f"in_{name}"] = a
        args.append(nc.dram_tensor(f"in_{name}", a.shape, mybir.dt.from_np(a.dtype), kind="ExternalInput").ap())
    out = nc.dram_tensor("out_y", (N + BLK, D), F32, kind="ExternalOutput").ap()
    vit_block(nc, *args, out)
    r = run_bass_kernel_spmd(nc, [arrays], core_ids=[0])
    return r.results[0]["out_y"][:N].reshape(IMAGES, SEQ, D)
```
